# Optimizing a Trainium2 kernel written in Bass

```python
import numpy as np
import jax
import jax.numpy as jnp

def _softmax(x, axis=-1):
    return jax.nn.softmax(x, axis=axis)

def _gelu(x):
    return jax.nn.gelu(x, approximate=True)

def _silu(x):
    return jax.nn.silu(x)

def _sigmoid(x):
    return jax.nn.sigmoid(x)

def _layernorm(x, axis=-1, eps=1e-05):
    m = jnp.mean(x, axis=axis, keepdims=True)
    v = jnp.var(x, axis=axis, keepdims=True)
    return (x - m) / jnp.sqrt(v + eps)

def _scatter_add(tgt, idx, src, axis=0):
    return tgt.at[idx].add(src)

def _segment_sum(src, seg, n):
    return jax.ops.segment_sum(src, seg, n)
kernel_name = 'mk_sandwich_d1_jaxref_r4_c8d6a5'

def setup_inputs(seed: int=0):
    np.random.seed(seed)
    _w = jnp.asarray

    def _L0_attn_setup():
        import jax, jax.numpy as jnp
        import numpy as np
        B, C, T = (32, 64, 1024)
        key = jax.random.key(seed)
        k1, k2 = jax.random.split(key)
        x = jax.random.normal(k1, (B, C, T), dtype=jnp.float32)
        gamma = jax.random.normal(k2, (1,), dtype=jnp.float32)
        return {'x': x, 'gamma': gamma}
    _L0_attn_in = _L0_attn_setup()

    def _L0_ffn_setup():
        import jax, jax.numpy as jnp
        import numpy as np
        LORA_RANK = 16
        LORA_ALPHA = 16
        LORA_SCALE = LORA_ALPHA / LORA_RANK
        key = jax.random.key(seed)
        k1, k2, k3, k4, k5 = jax.random.split(key, 5)
        B, S, D_IN, D_OUT, N_LORA, R = (8, 512, 1024, 1024, 3, LORA_RANK)
        std = 1.0 / np.sqrt(D_IN)
        x = jax.random.normal(k1, (B, S, D_IN), dtype=jnp.float32)
        weight = jax.random.truncated_normal(k2, -3.0, 3.0, (D_OUT, D_IN), dtype=jnp.float32) * std
        bias = jax.random.normal(k3, (D_OUT,), dtype=jnp.float32) * 0.01
        lora_A = jax.random.normal(k4, (N_LORA, R, D_IN), dtype=jnp.float32) * std
        lora_B = jax.random.normal(k5, (N_LORA, D_OUT, R), dtype=jnp.float32) * 0.02
        lora_start_indices = jnp.arange(4, dtype=jnp.int64) * 2
        return {'x': x, 'weight': weight, 'bias': bias, 'lora_A': lora_A, 'lora_B': lora_B, 'lora_start_indices': lora_start_indices}
    _L0_ffn_in = _L0_ffn_setup()
    _d = {'L0_attn_x': _L0_attn_in['x'], 'L0_attn_gamma': _L0_attn_in['gamma'], 'L0_ffn_weight': _L0_ffn_in['weight'], 'L0_ffn_bias': _L0_ffn_in['bias'], 'L0_ffn_lora_A': _L0_ffn_in['lora_A'], 'L0_ffn_lora_B': _L0_ffn_in['lora_B'], 'L0_ffn_lora_start_indices': _L0_ffn_in['lora_start_indices']}
    _x0 = _d['L0_attn_x']
    _d['L0_attn_x'] = jax.random.normal(jax.random.fold_in(jax.random.key(seed), 1), (2, 2048, 1024), dtype=_x0.dtype)
    del _x0
    return _d

def reference(L0_attn_x, L0_attn_gamma, L0_ffn_weight, L0_ffn_bias, L0_ffn_lora_A, L0_ffn_lora_B, L0_ffn_lora_start_indices):

    def _L0_attn_ref(x, gamma):
        import jax, jax.numpy as jnp
        import numpy as np
        B, C, T = (32, 64, 1024)
        energy = jnp.einsum('bit,bjt->bij', x, x)
        energy_new = jnp.max(energy, axis=-1, keepdims=True) - energy
        attention = jax.nn.softmax(energy_new, axis=-1)
        out = jnp.einsum('bij,bjt->bit', attention, x)
        return gamma * out + x

    def _L0_ffn_ref(x, weight, bias, lora_A, lora_B, lora_start_indices):
        import jax, jax.numpy as jnp
        import numpy as np
        LORA_RANK = 16
        LORA_ALPHA = 16
        LORA_SCALE = LORA_ALPHA / LORA_RANK
        y = jnp.einsum('bsd,od->bso', x, weight) + bias
        B = x.shape[0]
        seg = jnp.searchsorted(lora_start_indices, jnp.arange(B), side='right') - 1
        adapter_idx = jnp.clip(seg - 1, 0, lora_A.shape[0] - 1)
        A = lora_A[adapter_idx]
        Bw = lora_B[adapter_idx]
        lo = jnp.einsum('bsr,bor->bso', jnp.einsum('bsd,brd->bsr', x, A), Bw) * LORA_SCALE
        use_lora = (seg > 0)[:, None, None]
        return y + jnp.where(use_lora, lo, jnp.zeros((), dtype=y.dtype))
    x = L0_attn_x
    x = x + _layernorm(_L0_attn_ref(_layernorm(x, axis=-1), L0_attn_gamma), axis=-1)
    x = x + _layernorm(_L0_ffn_ref(_layernorm(x, axis=-1), L0_ffn_weight, L0_ffn_bias, L0_ffn_lora_A, L0_ffn_lora_B, L0_ffn_lora_start_indices), axis=-1)
    return x

_drawn_inputs = setup_inputs


def setup_inputs(seed=0):
    import zlib

    import numpy as np

    out = dict(_drawn_inputs(seed))
    spreads = {}
    factors = {'L0_ffn_bias': 8.0}
    for name, (base, spread) in spreads.items():
        noise = np.random.default_rng([zlib.crc32(name.encode()), seed]).standard_normal(out[name].shape)
        drawn = base * np.exp(spread * noise) if base else spread * noise
        out[name] = jnp.asarray(drawn.astype(out[name].dtype))
    for name, factor in factors.items():
        out[name] = (out[name] * factor).astype(out[name].dtype)
    return out
```

```python
from contextlib import ExitStack

import concourse.bass as bass
from concourse import mybir

ALU = mybir.AluOpType
ACT = mybir.ActivationFunctionType
AX = mybir.AxisListType
F32 = mybir.dt.float32
F16 = mybir.dt.float16
I32 = mybir.dt.int32

P = 128
BANK = 512
EPS = 1e-5
LN14 = 9.704060527839234
XS = 1024.0
WS = 256.0
DMA = 16


def sandwich(nc, x, gamma, weight, bias, lora_a, lora_b, starts, out):
    NB, S, D = x.shape
    NA, R, _ = lora_a.shape
    NT = S // P
    NK = D // P
    HT = NT // 2
    KR = NA * R
    NSTART = starts.shape[0]
    LAST = NB - 1
    assert NB == 2 and D == 2 * BANK and weight.shape[0] == D and NT == 16 and NSTART == 4 and NA == 3

    def chunks(j):
        return -(-(j + 1) // 4)

    ECHUNKS = sum(chunks(j) for j in range(NT))

    HEAD = 4
    order = []
    for j in range(NT):
        order.append(("E", j))
        if 1 <= j and j + HEAD - 1 < NT:
            order.append(("T", j + HEAD - 1))

    x_tiles = x.rearrange("b (t p) d -> (b t) p d", p=P)
    out_tiles = out.rearrange("b (t p) d -> (b t) p d", p=P)

    with ExitStack() as ctx:
        def sb(name, shape, dt):
            return ctx.enter_context(nc.sbuf_tensor(name, shape, dt))

        def sem(name):
            return ctx.enter_context(nc.semaphore(name))

        energy = sb("energy", [P, HT * (NT + 1), P], F32)
        x_high = sb("x_high", [P, NT, D], F16)
        x_low = sb("x_low", [P, NT, D], F16)
        region = sb("region", [P, NT * 2 * NK * P], F16)
        xt = region[:, :].rearrange("p (t s k n) -> p t s k n", t=NT, s=2, k=NK)
        TILE = 2 * NK * P

        def part(tile, n, dt):
            a = region[:, tile * TILE:(tile + n) * TILE]
            return a if dt == F16 else a.bitcast(dt)

        pt = part(1, 2, F16).rearrange("p (s j n) -> p s j n", s=2, j=NT)
        x1 = part(14, 2, F32).rearrange("p (r n) -> p r n", r=2)
        att = part(3, 1, F32)
        x2t = part(12, 1, F16).rearrange("p (s k n) -> p s k n", s=2, k=NK)
        y = part(13, 1, F32)
        p_below = part(0, 1, F32).rearrange("p (j n) -> p j n", n=P)
        wt = part(4, 8, F16).rearrange("p (s k n) -> p s k n", s=2, k=NK)
        w_stage = [part(13, 1, F32), part(12, 1, F32)]
        bt = part(3, 1, F32)[0:KR, :]
        a_mat = x1[0:KR, 1, :]
        flat = energy[:, :, :].rearrange("p b n -> p (b n)")
        x_in = [flat[:, P:P + D], flat[:, P + D:P + 2 * D]]
        xs = [flat[:, (NT + 1 + 2) * P:(NT + 1 + 2) * P + D],
              flat[:, (2 * (NT + 1) + 3) * P:(2 * (NT + 1) + 3) * P + D]]

        p_right = sb("p_right", [P, HT - 1, P], F32)
        b_raw = sb("b_raw", [P, NK, KR], F32)
        ident = sb("ident", [P, P], F32)
        bias_b = sb("bias_b", [P, D], F32)
        gamma_b = sb("gamma_b", [P, 1], F32)
        neg_half = sb("neg_half", [P, 1], F32)
        starts_i = sb("starts_i", [KR, NSTART], I32)
        starts_f = sb("starts_f", [KR, NSTART], F32)
        row_id = sb("row_id", [KR, 1], F32)
        below = sb("below", [KR, NB, NSTART], F32)
        seg = sb("seg", [KR, NB, 4], F32)
        mask = sb("mask", [KR, NB], F32)
        bn = sb("bn", [P, 4, 2, 6], F32)
        mv = sb("mv", [P, 4, 2], F32)
        veps = sb("veps", [P, 4], F32)
        x_r = sb("x_r", [P, NT], F32)
        x_nb = sb("x_nb", [P, NT], F32)
        ln_r = sb("ln_r", [P, 3], F32)
        ln_nb = sb("ln_nb", [P, 3], F32)
        emin = sb("emin", [P, NT, 6], F32)
        rmin = sb("rmin", [P, NT], F32)
        ebias = sb("ebias", [P, NT], F32)
        esum = sb("esum", [P, NT, 3], F32)
        rsum = sb("rsum", [P, NT], F32)
        rinv = sb("rinv", [P, NT], F32)
        coef = sb("coef", [P, NT], F32)

        ps_a = ctx.enter_context(nc.psum_tensor("ps_a", [P, 4 * BANK], F32))
        ps_b = ctx.enter_context(nc.psum_tensor("ps_b", [P, 2 * BANK], F32))
        ps_c = ctx.enter_context(nc.psum_tensor("ps_c", [P, 2 * BANK], F32))
        def ps_row(i, place, n):
            if i:
                return ps_a[:, place * P:(place + n) * P]
            return (ps_b if place < HT else ps_c)[:, place % HT * P:(place % HT + n) * P]

        ps_xt = [ps_b, ps_a[:, 0:2 * BANK], ps_a[:, 2 * BANK:4 * BANK], ps_b] + [(ps_c, ps_b)[t % 2] for t in range(HEAD, NT)]

        x_dma = [sem("x_dma0"), sem("x_dma1")]
        x_stats = sem("x_stats")
        x_norm = sem("x_norm")
        xs_done = sem("xs_done")
        xh_done = sem("xh_done")
        xl_done = sem("xl_done")
        xt_t = sem("xt_t")
        xth_done = sem("xth_done")
        xtl_done = sem("xtl_done")
        e_ps = sem("e_ps")
        e_kept = sem("e_kept")
        a_dma = sem("a_dma")
        b_dma = sem("b_dma")
        w_dma = [sem("w_dma0"), sem("w_dma1")]
        a_masked = sem("a_masked")
        bt_t = sem("bt_t")
        bt_done = sem("bt_done")
        lora_ps = sem("lora_ps")
        weff_done = sem("weff_done")
        wt_t = sem("wt_t")
        wh_done = sem("wh_done")
        wl_done = sem("wl_done")
        et_t = sem("et_t")
        eb_done = sem("eb_done")
        exp_done = sem("exp_done")
        pt_t = sem("pt_t")
        pth_done = sem("pth_done")
        ptl_done = sem("ptl_done")
        coef_done = sem("coef_done")
        pv_half = sem("pv_half")
        r_dma = [sem("r_dma0"), sem("r_dma1")]
        xs2_done = sem("xs2_done")
        att_evac = sem("att_evac")
        att_stats = sem("att_stats")
        att_norm = sem("att_norm")
        n_done = sem("n_done")
        x1_done = sem("x1_done")
        x1_stats = sem("x1_stats")
        x1_norm = sem("x1_norm")
        x2_done = sem("x2_done")
        x2t_t = sem("x2t_t")
        x2h_done = sem("x2h_done")
        x2l_done = sem("x2l_done")
        ffn_done = sem("ffn_done")
        y_evac = sem("y_evac")
        y_stats = sem("y_stats")
        y_norm = sem("y_norm")
        yn_done = sem("yn_done")
        out_ready = sem("out_ready")
        out_dma = sem("out_dma")
        bn_done = [sem(f"bn_done_{k}") for k in "xary"]
        veps_done = [sem(f"veps_done_{k}") for k in "xary"]
        r_done = [sem(f"r_done_{k}") for k in "xary"]
        emin_done = sem("emin_done")
        rmin_done = sem("rmin_done")
        rsum_done = sem("rsum_done")
        rinv_done = sem("rinv_done")
        const_dma = sem("const_dma")
        ident_zero = sem("ident_zero")
        const_ready = sem("const_ready")
        const_step = sem("const_step")
        bias_ready = sem("bias_ready")

        per_batch = {
            e_ps: ECHUNKS, e_kept: ECHUNKS, a_dma: DMA, a_masked: 1, bt_t: 1, bt_done: 1,
            lora_ps: 2 * NK, weff_done: 2 * NK, wt_t: 2 * NK, wh_done: 2 * NK, wl_done: 2 * NK,
            et_t: NT - 1, emin_done: NT - 1, pt_t: 2 * NT, pth_done: 2 * NT, ptl_done: 2 * NT, pv_half: 2 * NT,
            out_dma: DMA * NT,
        }
        for pair, n in ((x_dma, HT), (r_dma, HT), (w_dma, NK // 2)):
            per_batch.update({one: DMA * n for one in pair})
        primed = (y_evac, out_dma)

        XN, AN, RN, YN = range(4)

        def counts(b):
            def at(which, n):
                per = per_batch.get(which, NT)
                assert 0 <= n <= per, n
                return b * per + (n + 1 if which in primed else n)
            return at

        def block(j, i):
            return j * (NT + 1) + i if j < HT else (NT - 1 - j) * (NT + 1) + NT - j + i

        def slot(j):
            return NT - 1 - j if j >= HT else HT + j

        def columns(i):
            top = max(i + 1, HT)
            found = [(slot(NT - 1), NT - top, p_below[:, 0:NT - top, :])] if top < NT else []
            if i + 1 < HT:
                found.append((slot(i + 1), HT - 1 - i, p_right[:, i:HT - 1, :]))
            return found

        def p_block(i, j):
            if j <= i:
                return energy[:, block(i, j), :]
            return p_below[:, slot(j), :] if j >= HT else p_right[:, j - 1, :]

        block_of = ctx.enter_context(nc.Block())

        @block_of.sync
        def _(sp):
            sp.sem_inc(out_dma, 1)

            def load_x(t, b, at):
                if t >= 2:
                    sp.wait_ge(xs_done, at(xs_done, t - 1))
                sp.dma_start(x_in[t % 2], x_tiles[bass.ds(b * NT + t, 1), :, :].rearrange("a p d -> (a p) d"))\
                  .then_inc(x_dma[t % 2], DMA)

            for t in range(HEAD):
                load_x(t, 0, counts(0))
            sp.dma_start(starts_i[:, :], starts.rearrange("(a n) -> a n", a=1).to_broadcast([KR, NSTART])).then_inc(const_dma, DMA)
            sp.dma_start(gamma_b[:, :], gamma.rearrange("(a n) -> a n", a=1).to_broadcast([P, 1])).then_inc(const_dma, DMA)
            sp.dma_start(bias_b[:, :], bias.rearrange("(a n) -> a n", a=1).to_broadcast([P, D])).then_inc(const_dma, DMA)
            for t in range(HEAD, HEAD + 2):
                load_x(t, 0, counts(0))
            for a in range(NA):
                sp.dma_start(b_raw[:, :, a * R:(a + 1) * R], lora_b[a].rearrange("(t p) r -> p t r", p=P)).then_inc(b_dma, DMA)
            with sp.Fori(0, NB) as b:
                at = counts(b)
                for t in range(HEAD + 2, NT):
                    load_x(t, b, at)
                sp.wait_ge(e_ps, at(e_ps, ECHUNKS))
                sp.dma_start(a_mat, lora_a.rearrange("a r d -> (a r) d")).then_inc(a_dma, DMA)

                def load_w(w):
                    if w >= 2:
                        sp.wait_ge(wt_t, at(wt_t, 2 * (w - 1)))
                    sp.dma_start(w_stage[w % 2], weight[w * P:(w + 1) * P, :]).then_inc(w_dma[w % 2], DMA)

                def load_row(i):
                    if i == 1:
                        sp.wait_ge(lora_ps, at(lora_ps, 2 * NK))
                    sp.dma_start(x1[:, i % 2, :], x_tiles[bass.ds(b * NT + i, 1), :, :].rearrange("a p d -> (a p) d"))\
                      .then_inc(r_dma[i % 2], DMA)

                def store(i):
                    sp.wait_ge(out_ready, at(out_ready, i + 1))
                    sp.dma_start(out_tiles[bass.ds(b * NT + i, 1), :, :].rearrange("a p d -> (a p) d"), y)\
                      .then_inc(out_dma, DMA)

                load_w(0)
                load_w(1)
                load_row(0)
                for w in range(2, NK):
                    load_w(w)
                load_row(1)
                for i in range(NT - 3):
                    store(i)
                    load_row(i + 2)
                with sp.If(b < LAST):
                    sp.wait_ge(pt_t, at(pt_t, 2 * NT))
                    for t in range(2):
                        load_x(t, LAST, counts(LAST))
                store(NT - 3)
                load_row(NT - 1)
                with sp.If(b < LAST):
                    for t in range(2, HEAD):
                        load_x(t, LAST, counts(LAST))
                store(NT - 2)
                with sp.If(b < LAST):
                    for t in range(HEAD, HEAD + 2):
                        load_x(t, LAST, counts(LAST))
                store(NT - 1)
            sp.wait_ge(out_dma, NB * per_batch[out_dma] + 1)

        @block_of.tensor
        def _(pe):
            pe.wait_ge(const_ready, 2)

            def product(ps, left, right, first, last):
                for n, (u, v) in enumerate(((0, 0), (0, 1), (1, 0))):
                    mm = nc.tensor.matmul(ps, left[u], right[v], start=first and n == 0, stop=last and n == 2)
                return mm

            def transpose_x(t, at):
                pe.wait_ge(xs_done, at(xs_done, t + 1))
                if t == HEAD:
                    pe.wait_ge(y_evac, at(y_evac, 0))
                elif t == 3:
                    pe.wait_ge(xtl_done, at(xtl_done, 1))
                elif t > HEAD:
                    pe.wait_ge(xtl_done, at(xtl_done, t - 1))
                for k in range(NK):
                    tr = nc.tensor.transpose(ps_xt[t][:, k * P:(k + 1) * P], xs[t % 2][:, k * P:(k + 1) * P], ident[:, :])
                tr.then_inc(xt_t, 1)

            for t in range(HEAD):
                transpose_x(t, counts(0))
            with pe.Fori(0, NB) as b:
                at = counts(b)
                done = 0

                def energy_chunk(j, c):
                    nonlocal done
                    n = min(4, j + 1 - 4 * c)
                    if done >= 4:
                        pe.wait_ge(e_kept, at(e_kept, done - 3))
                    bank = ps_a[:, (done % 4) * BANK:(done % 4) * BANK + n * P]
                    for k in range(NK):
                        mm = product(bank, [xt[:, j, u, k, :] for u in range(2)],
                                     [xt[:, 4 * c:4 * c + n, u, k, :] for u in range(2)], k == 0, k == NK - 1)
                    mm.then_inc(e_ps, 1)
                    done += 1

                def energy_row(j):
                    pe.wait_ge(xtl_done, at(xtl_done, max(j, 2) + 1))
                    for c in range(chunks(j)):
                        energy_chunk(j, c)

                def transpose_b():
                    pe.wait_ge(b_dma, NA * DMA)
                    pe.wait_ge(ptl_done, at(ptl_done, 2))
                    pe.nop(nofuse=True)
                    for t in range(NK):
                        tr = nc.tensor.transpose(ps_c[0:KR, t * P:(t + 1) * P], b_raw[:, t, :], ident[:, :])
                    tr.then_inc(bt_t, 1)

                def lora(q):
                    w, h = q // 2, q % 2
                    if q == 0:
                        pe.wait_ge(bt_done, at(bt_done, 1))
                        pe.wait_ge(a_masked, at(a_masked, 1))
                    elif q > 1:
                        pe.wait_ge(wl_done, at(wl_done, q - 1))
                    nc.tensor.matmul(ps_c[:, h * BANK:(h + 1) * BANK], bt[:, w * P:(w + 1) * P],
                                     a_mat[:, h * BANK:(h + 1) * BANK], start=True, stop=True).then_inc(lora_ps, 1)

                def transpose_w(q):
                    w, h = q // 2, q % 2
                    pe.wait_ge(weff_done, at(weff_done, q + 1))
                    for k in range(h * HT // 2, (h + 1) * HT // 2):
                        tr = nc.tensor.transpose(ps_c[:, k * P:(k + 1) * P], w_stage[w % 2][:, k * P:(k + 1) * P], ident[:, :])
                    tr.then_inc(wt_t, 1)

                def prepare_weight(q):
                    if q:
                        transpose_w(q - 1)
                    if q < 2 * NK:
                        lora(q)

                def transpose_e(i):
                    if i == 0:
                        pe.wait_ge(e_kept, at(e_kept, ECHUNKS - 3))
                    elif i == 1:
                        pe.wait_ge(e_kept, at(e_kept, ECHUNKS))
                    else:
                        pe.wait_ge(ptl_done, at(ptl_done, 2 * i))
                    if i == NT - 1:
                        return
                    for j in range(i + 1, NT):
                        tr = nc.tensor.transpose(ps_row(i, slot(j), 1), energy[:, block(j, i), :], ident[:, :])
                    tr.then_inc(et_t, 1)

                def transpose_p(i, h):
                    pe.wait_ge(exp_done, at(exp_done, i + 1))
                    for j in range(h * HT, (h + 1) * HT):
                        tr = nc.tensor.transpose(ps_row(i, j, 1), p_block(i, j), ident[:, :])
                    tr.then_inc(pt_t, 1)

                def attend(i, h):
                    pe.wait_ge(ptl_done, at(ptl_done, 2 * i + h + 1))
                    if h == 0:
                        if i:
                            pe.wait_ge(att_evac, at(att_evac, i))
                        else:
                            pe.wait_ge(xl_done, at(xl_done, NT))
                            pe.wait_ge(ptl_done, at(ptl_done, 2))
                    for j in range(h * HT, (h + 1) * HT):
                        for c in range(2):
                            mm = product(ps_b[:, c * BANK:(c + 1) * BANK], [pt[:, u, j, :] for u in range(2)],
                                         [z[:, j, c * BANK:(c + 1) * BANK] for z in (x_high, x_low)], j == 0, j == NT - 1)
                        if j == (h + 1) * HT - 1:
                            mm.then_inc(pv_half, 1)
                        if i == 0 and j >= 2:
                            prepare_weight(j - 2)

                def transpose_x2(i):
                    pe.wait_ge(x2_done, at(x2_done, i + 1))
                    if i:
                        pe.wait_ge(y_evac, at(y_evac, i))
                    else:
                        pe.wait_ge(wl_done, at(wl_done, 2 * NK))
                    for k in range(NK):
                        tr = nc.tensor.transpose(ps_c[:, k * P:(k + 1) * P], att[:, k * P:(k + 1) * P], ident[:, :])
                    tr.then_inc(x2t_t, 1)

                def feed_forward(i):
                    pe.wait_ge(x2l_done, at(x2l_done, i + 1))
                    for c in range(2):
                        for k in range(NK):
                            mm = product(ps_c[:, c * BANK:(c + 1) * BANK], [x2t[:, u, k, :] for u in range(2)],
                                         [wt[:, u, k, c * BANK:(c + 1) * BANK] for u in range(2)], k == 0, k == NK - 1)
                    mm.then_inc(ffn_done, 1)

                for kind, n in order[:-1]:
                    if kind == "T":
                        transpose_x(n, at)
                    else:
                        energy_row(n)
                pe.wait_ge(xtl_done, at(xtl_done, NT))
                energy_chunk(NT - 1, 0)
                energy_chunk(NT - 1, 1)
                transpose_e(0)
                energy_chunk(NT - 1, 2)
                transpose_p(0, 0)
                transpose_p(0, 1)
                energy_chunk(NT - 1, 3)
                transpose_b()
                for i in range(NT):
                    if i + 1 < NT:
                        transpose_e(i + 1)
                    attend(i, 0)
                    if i + 1 < NT:
                        transpose_p(i + 1, 0)
                    if i:
                        transpose_x2(i - 1)
                    attend(i, 1)
                    if i + 1 < NT:
                        transpose_p(i + 1, 1)
                    if i == 0:
                        for q in range(NT - 2, 2 * NK + 1):
                            prepare_weight(q)
                    if i:
                        feed_forward(i - 1)
                with pe.If(b < LAST):
                    pe.wait_ge(att_evac, at(att_evac, NT))
                    transpose_x(0, counts(LAST))
                    transpose_x(1, counts(LAST))
                transpose_x2(NT - 1)
                with pe.If(b < LAST):
                    transpose_x(2, counts(LAST))
                feed_forward(NT - 1)
                with pe.If(b < LAST):
                    transpose_x(3, counts(LAST))

        @block_of.vector
        def _(dve):
            dve.sem_inc(y_evac, 1)

            def row_stats(kind, n, rows, done, at):
                nc.vector.bn_stats(bn[:, kind, 0, :], rows[:, 0:BANK])
                nc.vector.bn_stats(bn[:, kind, 1, :], rows[:, BANK:D]).then_inc(bn_done[kind], 1)
                dve.wait_ge(bn_done[kind], at(bn_done[kind], n + 1))
                dve.nop(nofuse=True)
                nc.vector.bn_aggr(mv[:, kind, :], bn[:, kind, :, :]).then_inc(done, 1)

            def stats_x(t, at):
                dve.wait_ge(x_dma[t % 2], at(x_dma[t % 2], DMA * (t // 2 + 1)))
                if t:
                    dve.wait_ge(x_norm, at(x_norm, t))
                row_stats(XN, t, x_in[t % 2], x_stats, at)

            def split_xt(t, at):
                dve.wait_ge(xth_done, at(xth_done, t + 1))
                nc.vector.tensor_tensor(xt[:, t, 1, :, :].rearrange("p k n -> p (k n)"), ps_xt[t][:, :],
                                        xt[:, t, 0, :, :].rearrange("p k n -> p (k n)"), ALU.subtract).then_inc(xtl_done, 1)

            stats_x(0, counts(0))
            for t in range(HEAD):
                if t + 1 < HEAD:
                    stats_x(t + 1, counts(0))
                if t:
                    split_xt(t - 1, counts(0))
            stats_x(HEAD, counts(0))
            split_xt(HEAD - 1, counts(0))

            count = [0]

            dve.wait_ge(const_dma, 3 * DMA)
            dve.wait_ge(const_ready, 2)

            def const(ins):
                count[0] += 1
                ins.then_inc(const_step, 1)
                dve.wait_ge(const_step, count[0])

            const(nc.vector.tensor_copy(starts_f[:, :], starts_i[:, :]))
            for n in range(NB):
                lo, hi = below[:, n, :], seg[:, n, :]
                const(nc.vector.tensor_scalar(lo, starts_f[:, :], float(n), None, ALU.is_le))
                const(nc.vector.tensor_scalar(hi[:, 0:1], lo[:, 0:1], -1.0, 2.0, ALU.mult, ALU.add))
                const(nc.vector.scalar_tensor_tensor(hi[:, 1:2], hi[:, 0:1], lo[:, 1:2], lo[:, 0:1], ALU.mult, ALU.add))
                const(nc.vector.scalar_tensor_tensor(hi[:, 2:3], lo[:, 3:4], 3.0, hi[:, 1:2], ALU.add, ALU.subtract))
                const(nc.vector.scalar_tensor_tensor(hi[:, 3:4], hi[:, 2:3], lo[:, 2:3], hi[:, 1:2], ALU.mult, ALU.add))
                const(nc.vector.scalar_tensor_tensor(hi[:, 0:1], hi[:, 3:4], -float(R), row_id[:, :], ALU.mult, ALU.add))
                const(nc.vector.tensor_scalar(hi[:, 1:2], hi[:, 0:1], -2.0 * R, None, ALU.is_ge))
                const(nc.vector.scalar_tensor_tensor(mask[:, n:n + 1], hi[:, 0:1], float(-R), hi[:, 1:2], ALU.is_lt, ALU.mult))
            nc.vector.tensor_scalar(bias_b[:, :], bias_b[:, :], XS * WS, None, ALU.mult).then_inc(bias_ready, 1)
            dve.wait_ge(bias_ready, 1)

            with dve.Fori(0, NB) as b:
                at = counts(b)
                done = 0

                def keep_chunk(j, c):
                    nonlocal done
                    n = min(4, j + 1 - 4 * c)
                    dve.wait_ge(e_ps, at(e_ps, done + 1))
                    place = block(j, 4 * c)
                    nc.vector.tensor_scalar(flat[:, place * P:(place + n) * P], ps_a[:, (done % 4) * BANK:(done % 4) * BANK + n * P],
                                            1.0, None, ALU.mult, ALU.min, accum_out=emin[:, j, c:c + 1]).then_inc(e_kept, 1)
                    done += 1

                def keep_energy(j):
                    if j >= NT - 3:
                        dve.wait_ge(xt_t, at(xt_t, NT))
                        dve.wait_ge(xl_done, at(xl_done, NT))
                    for c in range(chunks(j)):
                        keep_chunk(j, c)

                stats_x(HEAD + 1, at)
                for kind, n in order[:-1]:
                    if kind == "T":
                        split_xt(n, at)
                        if n + 2 < NT:
                            stats_x(n + 2, at)
                    else:
                        keep_energy(n)
                keep_chunk(NT - 1, 0)
                keep_chunk(NT - 1, 1)

                def row_minimum(i):
                    parts = chunks(i)
                    if i < NT - 1:
                        dve.wait_ge(et_t, at(et_t, i + 1))
                        for p0, n, _ in columns(i):
                            last = nc.vector.tensor_reduce(emin[:, i, parts:parts + 1], ps_row(i, p0, n), AX.X, ALU.min)
                            parts += 1
                        last.then_inc(emin_done, 1)
                        dve.wait_ge(emin_done, at(emin_done, i + 1))
                    else:
                        dve.wait_ge(e_kept, at(e_kept, ECHUNKS))
                    nc.vector.tensor_reduce(rmin[:, i:i + 1], emin[:, i, 0:parts], AX.X, ALU.min).then_inc(rmin_done, 1)
                    dve.wait_ge(rmin_done, at(rmin_done, i + 1))
                    nc.vector.tensor_scalar(ebias[:, i:i + 1], rmin[:, i:i + 1], 1.0 / (XS * XS), LN14, ALU.mult, ALU.add)\
                      .then_inc(eb_done, 1)

                def coefficient(i):
                    dve.wait_ge(exp_done, at(exp_done, i + 1))
                    parts = 1 + len(columns(i))
                    nc.vector.tensor_reduce(rsum[:, i:i + 1], esum[:, i, 0:parts], AX.X, ALU.add).then_inc(rsum_done, 1)
                    dve.wait_ge(rsum_done, at(rsum_done, i + 1))
                    nc.vector.reciprocal(rinv[:, i:i + 1], rsum[:, i:i + 1]).then_inc(rinv_done, 1)
                    dve.wait_ge(rinv_done, at(rinv_done, i + 1))
                    nc.vector.tensor_tensor(coef[:, i:i + 1], rinv[:, i:i + 1], gamma_b[:, :], ALU.mult).then_inc(coef_done, 1)

                def split_pt(i, h):
                    dve.wait_ge(pth_done, at(pth_done, 2 * i + h + 1))
                    a, z = h * HT, (h + 1) * HT
                    nc.vector.tensor_tensor(pt[:, 1, a:z, :].rearrange("p j n -> p (j n)"), ps_row(i, a, HT),
                                            pt[:, 0, a:z, :].rearrange("p j n -> p (j n)"), ALU.subtract).then_inc(ptl_done, 1)

                def mask_adapters():
                    dve.wait_ge(bt_t, at(bt_t, 1))
                    nc.vector.tensor_copy(bt, ps_c[0:KR, :]).then_inc(bt_done, 1)
                    dve.wait_ge(a_dma, at(a_dma, DMA))
                    nc.vector.tensor_scalar(a_mat, a_mat, mask[:, bass.ds(b, 1)], None, ALU.mult).then_inc(a_masked, 1)

                def add_adapter(q):
                    w, h = q // 2, q % 2
                    dve.wait_ge(w_dma[w % 2], at(w_dma[w % 2], DMA * (w // 2 + 1)))
                    dve.wait_ge(lora_ps, at(lora_ps, q + 1))
                    half = w_stage[w % 2][:, h * BANK:(h + 1) * BANK]
                    nc.vector.tensor_tensor(half, ps_c[:, h * BANK:(h + 1) * BANK], half, ALU.add).then_inc(weff_done, 1)

                def split_weight(q):
                    w, k = q // 2, q % 2 * (NK // 2)
                    dve.wait_ge(wh_done, at(wh_done, q + 1))
                    nc.vector.scalar_tensor_tensor(wt[:, 1, k:k + NK // 2, w * P:(w + 1) * P],
                                                   ps_c[:, k * P:k * P + BANK].rearrange("p (k n) -> p k n", k=NK // 2), WS,
                                                   wt[:, 0, k:k + NK // 2, w * P:(w + 1) * P], ALU.mult, ALU.subtract).then_inc(wl_done, 1)

                def prepare_weight(first, end):
                    for q in range(first, end):
                        if q < 2 * NK:
                            add_adapter(q)
                        if q:
                            split_weight(q - 1)

                def attended(i):
                    dve.wait_ge(pv_half, at(pv_half, 2 * i + 2))
                    dve.wait_ge(xs2_done, at(xs2_done, i + 1))
                    dve.wait_ge(coef_done, at(coef_done, i + 1))
                    nc.vector.scalar_tensor_tensor(att, ps_b[:, :], coef[:, i:i + 1], att, ALU.mult, ALU.add)\
                      .then_inc(att_evac, 1)
                    dve.wait_ge(att_evac, at(att_evac, i + 1))
                    if i:
                        dve.wait_ge(att_norm, at(att_norm, i))
                    row_stats(AN, i, att, att_stats, at)

                def stats_x1(i):
                    dve.wait_ge(x1_done, at(x1_done, i + 1))
                    if i:
                        dve.wait_ge(x1_norm, at(x1_norm, i))
                    row_stats(RN, i, x1[:, i % 2, :], x1_stats, at)

                def split_x2(i):
                    dve.wait_ge(x2h_done, at(x2h_done, i + 1))
                    nc.vector.tensor_tensor(x2t[:, 1, :, :].rearrange("p k n -> p (k n)"), ps_c[:, :],
                                            x2t[:, 0, :, :].rearrange("p k n -> p (k n)"), ALU.subtract).then_inc(x2l_done, 1)

                def stats_y(i):
                    dve.wait_ge(ffn_done, at(ffn_done, i + 1))
                    if i:
                        dve.wait_ge(out_dma, at(out_dma, DMA * i))
                        dve.wait_ge(y_norm, at(y_norm, i))
                    nc.vector.tensor_tensor(y, ps_c[:, :], bias_b[:, :], ALU.add).then_inc(y_evac, 1)
                    dve.wait_ge(y_evac, at(y_evac, i + 1))
                    row_stats(YN, i, y, y_stats, at)

                row_minimum(0)
                keep_chunk(NT - 1, 2)
                split_pt(0, 0)
                split_pt(0, 1)
                keep_chunk(NT - 1, 3)
                mask_adapters()
                for i in range(NT - 1):
                    if i >= 2:
                        stats_y(i - 2)
                    row_minimum(i + 1)
                    if i == 0:
                        prepare_weight(0, HT - 2)
                    split_pt(i + 1, 0)
                    if i:
                        split_x2(i - 1)
                    else:
                        prepare_weight(HT - 2, NT - 2)
                    coefficient(i)
                    if i == 0:
                        split_pt(1, 1)
                        prepare_weight(NT - 2, 2 * NK + 1)
                    attended(i)
                    if i:
                        split_pt(i + 1, 1)
                    stats_x1(i)
                stats_y(NT - 3)
                split_x2(NT - 2)
                coefficient(NT - 1)
                with dve.If(b < LAST):
                    stats_x(0, counts(LAST))
                    stats_x(1, counts(LAST))
                attended(NT - 1)
                with dve.If(b < LAST):
                    stats_x(2, counts(LAST))
                stats_x1(NT - 1)
                stats_y(NT - 2)
                with dve.If(b < LAST):
                    split_xt(0, counts(LAST))
                    stats_x(3, counts(LAST))
                split_x2(NT - 1)
                with dve.If(b < LAST):
                    split_xt(1, counts(LAST))
                    split_xt(2, counts(LAST))
                    stats_x(4, counts(LAST))
                    split_xt(3, counts(LAST))
                stats_y(NT - 1)

        @block_of.scalar
        def _(act):
            def norm_x(t, at):
                act.wait_ge(x_norm, at(x_norm, t + 1))
                if t >= 2:
                    act.wait_ge(xt_t, at(xt_t, t - 1))
                    act.wait_ge(xl_done, at(xl_done, t - 1))
                nc.scalar.activation(xs[t % 2], x_in[t % 2], ACT.Identity, bias=x_nb[:, t:t + 1], scale=x_r[:, t:t + 1])\
                  .then_inc(xs_done, 1)

            def high_x(t, at):
                act.wait_ge(xs_done, at(xs_done, t + 1))
                nc.scalar.activation(x_high[:, t, :], xs[t % 2], ACT.Copy).then_inc(xh_done, 1)

            def split_xt(t, at):
                act.wait_ge(xt_t, at(xt_t, t + 1))
                if t == NT - 3:
                    act.wait_ge(out_dma, at(out_dma, 0))
                nc.scalar.activation(xt[:, t, 0, :, :].rearrange("p k n -> p (k n)"), ps_xt[t][:, :], ACT.Copy)\
                  .then_inc(xth_done, 1)

            norm_x(0, counts(0))
            for t in range(HEAD):
                high_x(t, counts(0))
                if t + 1 < HEAD:
                    norm_x(t + 1, counts(0))
                split_xt(t, counts(0))
            norm_x(HEAD, counts(0))
            high_x(HEAD, counts(0))
            with act.Fori(0, NB) as b:
                at = counts(b)
                for kind, t in order:
                    if kind == "T":
                        split_xt(t, at)
                        if t + 1 < NT:
                            norm_x(t + 1, at)
                            high_x(t + 1, at)

                def exponentials(i):
                    act.wait_ge(eb_done, at(eb_done, i + 1))
                    row = flat[:, block(i, 0) * P:(block(i, 0) + i + 1) * P]
                    pieces = [(row, row)]
                    for p0, n, place in columns(i):
                        pieces.append((place, ps_row(i, p0, n).rearrange("p (j n) -> p j n", n=P)))
                    for n, (dst, src) in enumerate(pieces):
                        e = nc.scalar.activation(dst, src, ACT.Exp, bias=ebias[:, i:i + 1], scale=-1.0 / (XS * XS),
                                                 accum_out=esum[:, i, n:n + 1])
                    e.then_inc(exp_done, 1)

                def split_pt(i, h):
                    act.wait_ge(pt_t, at(pt_t, 2 * i + h + 1))
                    if i:
                        act.wait_ge(pv_half, at(pv_half, 2 * i - 1 + h))
                    a, z = h * HT, (h + 1) * HT
                    nc.scalar.activation(pt[:, 0, a:z, :].rearrange("p j n -> p (j n)"), ps_row(i, a, HT), ACT.Copy)\
                      .then_inc(pth_done, 1)

                def high_weight(first, end):
                    for q in range(first, end):
                        w, k = q // 2, q % 2 * (NK // 2)
                        act.wait_ge(wt_t, at(wt_t, q + 1))
                        if q == 0:
                            act.wait_ge(e_ps, at(e_ps, ECHUNKS))
                        nc.scalar.activation(wt[:, 0, k:k + NK // 2, w * P:(w + 1) * P],
                                             ps_c[:, k * P:k * P + BANK].rearrange("p (k n) -> p k n", k=NK // 2), ACT.Copy,
                                             scale=WS).then_inc(wh_done, 1)

                def norm_rows(i):
                    act.wait_ge(r_dma[i % 2], at(r_dma[i % 2], DMA * (i // 2 + 1)))
                    if i:
                        act.wait_ge(x2t_t, at(x2t_t, i))
                    else:
                        act.wait_ge(lora_ps, at(lora_ps, 2 * NK))
                    nc.scalar.activation(att, x1[:, i % 2, :], ACT.Identity, bias=x_nb[:, i:i + 1], scale=x_r[:, i:i + 1])\
                      .then_inc(xs2_done, 1)

                def split_x2(i):
                    act.wait_ge(x2t_t, at(x2t_t, i + 1))
                    if i:
                        act.wait_ge(ffn_done, at(ffn_done, i))
                    else:
                        act.wait_ge(wt_t, at(wt_t, 2 * NK))
                    nc.scalar.activation(x2t[:, 0, :, :].rearrange("p k n -> p (k n)"), ps_c[:, :], ACT.Copy).then_inc(x2h_done, 1)

                def norm_attended(i):
                    act.wait_ge(att_norm, at(att_norm, i + 1))
                    nc.scalar.activation(att, att, ACT.Identity, bias=ln_nb[:, 0:1], scale=ln_r[:, 0:1]).then_inc(n_done, 1)

                def norm_x1(i):
                    act.wait_ge(x1_norm, at(x1_norm, i + 1))
                    nc.scalar.activation(att, x1[:, i % 2, :], ACT.Identity, bias=ln_nb[:, 1:2], scale=ln_r[:, 1:2])\
                      .then_inc(x2_done, 1)

                def norm_y(i):
                    act.wait_ge(y_norm, at(y_norm, i + 1))
                    nc.scalar.activation(y, y, ACT.Identity, bias=ln_nb[:, 2:3], scale=ln_r[:, 2:3]).then_inc(yn_done, 1)

                exponentials(0)
                split_pt(0, 0)
                split_pt(0, 1)
                for i in range(NT - 1):
                    if i >= 2:
                        norm_y(i - 2)
                    exponentials(i + 1)
                    if i == 0:
                        high_weight(0, HT - 3)
                    split_pt(i + 1, 0)
                    if i:
                        split_x2(i - 1)
                    else:
                        high_weight(HT - 3, NT - 3)
                        split_pt(1, 1)
                        high_weight(NT - 3, 2 * NK)
                    norm_rows(i)
                    if i:
                        split_pt(i + 1, 1)
                    norm_attended(i)
                    norm_x1(i)
                norm_y(NT - 3)
                split_x2(NT - 2)
                norm_rows(NT - 1)
                with act.If(b < LAST):
                    norm_x(0, counts(LAST))
                    norm_x(1, counts(LAST))
                norm_attended(NT - 1)
                with act.If(b < LAST):
                    act.wait_ge(pv_half, at(pv_half, 2 * NT))
                    high_x(0, counts(LAST))
                norm_x1(NT - 1)
                with act.If(b < LAST):
                    high_x(1, counts(LAST))
                    split_xt(0, counts(LAST))
                    norm_x(2, counts(LAST))
                split_x2(NT - 1)
                norm_y(NT - 2)
                with act.If(b < LAST):
                    split_xt(1, counts(LAST))
                    high_x(2, counts(LAST))
                    norm_x(3, counts(LAST))
                    split_xt(2, counts(LAST))
                    high_x(3, counts(LAST))
                    norm_x(4, counts(LAST))
                    split_xt(3, counts(LAST))
                    high_x(4, counts(LAST))
                norm_y(NT - 1)

        @block_of.gpsimd
        def _(pool):
            nc.gpsimd.memset(ident[:, :], 0.0).then_inc(ident_zero, 1)
            nc.gpsimd.memset(neg_half[:, :], -0.5)
            nc.gpsimd.iota(row_id[:, :], [[0, 1]], base=0, channel_multiplier=1, allow_small_or_imprecise_dtypes=True).then_inc(const_ready, 1)
            pool.wait_ge(ident_zero, 1)
            nc.gpsimd.affine_select(out=ident[:, :], in_=ident[:, :], compare_op=ALU.not_equal, fill=1.0,
                                    base=0, pattern=[[-1, P]], channel_multiplier=1).then_inc(const_ready, 1)
            pool.wait_ge(const_ready, 2)

            def norm(kind, n, scale, eps, r, nb, done, at):
                pool.nop(nofuse=True)
                nc.gpsimd.tensor_scalar(veps[:, kind:kind + 1], mv[:, kind, 1:2], scale, eps, ALU.mult, ALU.add)\
                  .then_inc(veps_done[kind], 1)
                pool.wait_ge(veps_done[kind], at(veps_done[kind], n + 1))
                nc.gpsimd.tensor_tensor(r, veps[:, kind:kind + 1], neg_half[:, :], ALU.pow).then_inc(r_done[kind], 1)
                pool.wait_ge(r_done[kind], at(r_done[kind], n + 1))
                pool.nop(nofuse=True)
                nc.gpsimd.tensor_scalar(nb, mv[:, kind, 0:1], r, -1.0, ALU.mult, ALU.mult).then_inc(done, 1)

            def norm_x(t, at):
                pool.wait_ge(x_stats, at(x_stats, t + 1))
                norm(XN, t, XS ** -2, EPS * XS ** -2, x_r[:, t:t + 1], x_nb[:, t:t + 1], x_norm, at)

            def low_x(t, at):
                pool.wait_ge(xh_done, at(xh_done, t + 1))
                nc.gpsimd.tensor_tensor(x_low[:, t, :], xs[t % 2], x_high[:, t, :], ALU.subtract).then_inc(xl_done, 1)

            norm_x(0, counts(0))
            norm_x(1, counts(0))
            for t in range(HEAD):
                low_x(t, counts(0))
                if t + 2 <= HEAD:
                    norm_x(t + 2, counts(0))
            with pool.Fori(0, NB) as b:
                at = counts(b)
                norm_x(HEAD + 1, at)
                for t in range(HEAD, NT):
                    low_x(t, at)
                    if t + 2 < NT:
                        norm_x(t + 2, at)

                def finish_y(i):
                    pool.wait_ge(y_stats, at(y_stats, i + 1))
                    norm(YN, i, 1.0, EPS * (XS * WS) ** 2, ln_r[:, 2:3], ln_nb[:, 2:3], y_norm, at)
                    pool.wait_ge(yn_done, at(yn_done, i + 1))
                    nc.gpsimd.tensor_tensor(y, x1[:, i % 2, :], y, ALU.add).then_inc(out_ready, 1)

                def residual(i):
                    pool.wait_ge(att_stats, at(att_stats, i + 1))
                    norm(AN, i, 1.0, EPS * XS ** 2, ln_r[:, 0:1], ln_nb[:, 0:1], att_norm, at)
                    pool.wait_ge(n_done, at(n_done, i + 1))
                    nc.gpsimd.tensor_tensor(x1[:, i % 2, :], x1[:, i % 2, :], att, ALU.add).then_inc(x1_done, 1)

                def norm_residual(i):
                    pool.wait_ge(x1_stats, at(x1_stats, i + 1))
                    norm(RN, i, XS ** -2, EPS * XS ** -2, ln_r[:, 1:2], ln_nb[:, 1:2], x1_norm, at)

                for i in range(NT - 1):
                    if i >= 2:
                        finish_y(i - 2)
                    residual(i)
                    norm_residual(i)
                finish_y(NT - 3)
                with pool.If(b < LAST):
                    norm_x(0, counts(LAST))
                    norm_x(1, counts(LAST))
                residual(NT - 1)
                with pool.If(b < LAST):
                    norm_x(2, counts(LAST))
                norm_residual(NT - 1)
                with pool.If(b < LAST):
                    low_x(0, counts(LAST))
                    low_x(1, counts(LAST))
                    norm_x(3, counts(LAST))
                finish_y(NT - 2)
                with pool.If(b < LAST):
                    low_x(2, counts(LAST))
                    low_x(3, counts(LAST))
                    norm_x(4, counts(LAST))
                finish_y(NT - 1)


_INS = ["L0_attn_x", "L0_attn_gamma", "L0_ffn_weight", "L0_ffn_bias", "L0_ffn_lora_A", "L0_ffn_lora_B",
        "L0_ffn_lora_start_indices"]


def kernel(**inputs):
    import numpy as np
    import concourse.bacc as bacc
    from concourse.bass_utils import run_bass_kernel_spmd

    nc = bacc.Bacc("TRN2", target_bir_lowering=False, num_devices=1)
    arrays, args = {}, []
    for name in _INS:
        a = np.ascontiguousarray(inputs[name])
        arrays[f"in_{name}"] = a
        args.append(nc.dram_tensor(f"in_{name}", a.shape, mybir.dt.from_np(a.dtype), kind="ExternalInput").ap())
    shape = inputs["L0_attn_x"].shape
    args.append(nc.dram_tensor("out_x", shape, F32, kind="ExternalOutput").ap())
    sandwich(nc, *args)
    r = run_bass_kernel_spmd(nc, [arrays], core_ids=[0])
    return r.results[0]["out_x"]
```

```python
from contextlib import ExitStack

import concourse.bass as bass
from concourse import mybir

ALU = mybir.AluOpType
ACT = mybir.ActivationFunctionType
AX = mybir.AxisListType
F32 = mybir.dt.float32
F16 = mybir.dt.float16
I32 = mybir.dt.int32

P = 128
BANK = 512
EPS = 1e-5
LN14 = 9.704060527839234
XS = 1024.0
WS = 256.0
DMA = 16


def sandwich(nc, x, gamma, weight, bias, lora_a, lora_b, starts, out):
    NB, S, D = x.shape
    NA, R, _ = lora_a.shape
    NT = S // P
    NK = D // P
    HT = NT // 2
    KR = NA * R
    NSTART = starts.shape[0]
    LAST = NB - 1
    assert NB == 2 and D == 2 * BANK and weight.shape[0] == D and NT == 16 and NSTART == 4 and NA == 3

    def chunks(j):
        return -(-(j + 1) // 4)

    ECHUNKS = sum(chunks(j) for j in range(NT))

    HEAD = 4
    order = []
    for j in range(NT):
        order.append(("E", j))
        if 1 <= j and j + HEAD - 1 < NT:
            order.append(("T", j + HEAD - 1))

    x_tiles = x.rearrange("b (t p) d -> (b t) p d", p=P)
    out_tiles = out.rearrange("b (t p) d -> (b t) p d", p=P)

    with ExitStack() as ctx:
        def sb(name, shape, dt):
            return ctx.enter_context(nc.sbuf_tensor(name, shape, dt))

        def sem(name):
            return ctx.enter_context(nc.semaphore(name))

        energy = sb("energy", [P, HT * (NT + 1), P], F32)
        x_high = sb("x_high", [P, NT, D], F16)
        x_low = sb("x_low", [P, NT, D], F16)
        region = sb("region", [P, NT * 2 * NK * P], F16)
        xt = region[:, :].rearrange("p (t s k n) -> p t s k n", t=NT, s=2, k=NK)
        TILE = 2 * NK * P

        def part(tile, n, dt):
            a = region[:, tile * TILE:(tile + n) * TILE]
            return a if dt == F16 else a.bitcast(dt)

        pt = part(1, 2, F16).rearrange("p (s j n) -> p s j n", s=2, j=NT)
        x1 = part(14, 2, F32).rearrange("p (r n) -> p r n", r=2)
        att = part(3, 1, F32)
        x2t = part(12, 1, F16).rearrange("p (s k n) -> p s k n", s=2, k=NK)
        y = part(13, 1, F32)
        p_below = part(0, 1, F32).rearrange("p (j n) -> p j n", n=P)
        wt = part(4, 8, F16).rearrange("p (s k n) -> p s k n", s=2, k=NK)
        w_stage = [part(13, 1, F32), part(12, 1, F32)]
        bt = part(3, 1, F32)[0:KR, :]
        a_mat = x1[0:KR, 1, :]
        flat = energy[:, :, :].rearrange("p b n -> p (b n)")
        x_in = [flat[:, P:P + D], flat[:, P + D:P + 2 * D]]
        xs = [flat[:, (NT + 1 + 2) * P:(NT + 1 + 2) * P + D],
              flat[:, (2 * (NT + 1) + 3) * P:(2 * (NT + 1) + 3) * P + D]]

        p_right = sb("p_right", [P, HT - 1, P], F32)
        b_raw = sb("b_raw", [P, NK, KR], F32)
        col_min = sb("col_min", [P, 2, P], F32)
        ones = sb("ones", [P, 1], F16)
        ln14 = sb("ln14", [P, 1], F32)
        ident = sb("ident", [P, P], F32)
        bias_b = sb("bias_b", [P, D], F32)
        gamma_b = sb("gamma_b", [P, 1], F32)
        neg_half = sb("neg_half", [P, 1], F32)
        starts_i = sb("starts_i", [KR, NSTART], I32)
        starts_f = sb("starts_f", [KR, NSTART], F32)
        row_id = sb("row_id", [KR, 1], F32)
        is_below = sb("is_below", [KR, NB, NSTART], F32)
        seg = sb("seg", [KR, NB, 4], F32)
        mask = sb("mask", [KR, NB], F32)
        bn = sb("bn", [P, 4, 2, 6], F32)
        mv = sb("mv", [P, 4, 2], F32)
        veps = sb("veps", [P, 4], F32)
        x_r = sb("x_r", [P, NT], F32)
        x_nb = sb("x_nb", [P, NT], F32)
        ln_r = sb("ln_r", [P, 3], F32)
        ln_nb = sb("ln_nb", [P, 3], F32)
        emin = sb("emin", [P, NT, 5], F32)
        rmin = sb("rmin", [P, NT], F32)
        ebias = sb("ebias", [P, NT], F32)
        esum = sb("esum", [P, NT], F32)
        rsum = sb("rsum", [P, 2], F32)
        rinv = sb("rinv", [P, 2], F32)
        coef = sb("coef", [P, 2], F32)

        ps_a = ctx.enter_context(nc.psum_tensor("ps_a", [P, 4 * BANK], F32))
        ps_b = ctx.enter_context(nc.psum_tensor("ps_b", [P, 2 * BANK], F32))
        ps_c = ctx.enter_context(nc.psum_tensor("ps_c", [P, 2 * BANK], F32))
        def ps_row(i, place, n):
            if i:
                return ps_a[:, place * P:(place + n) * P]
            return (ps_b if place < HT else ps_c)[:, place % HT * P:(place % HT + n) * P]

        ps_xt = [ps_b, ps_a[:, 0:2 * BANK], ps_a[:, 2 * BANK:4 * BANK], ps_b] + [(ps_c, ps_b)[t % 2] for t in range(HEAD, NT)]

        def block(j, i):
            return j * (NT + 1) + i if j < HT else (NT - 1 - j) * (NT + 1) + NT - j + i

        def slot(j):
            return NT - 1 - j if j >= HT else HT + j

        def below(i):
            found = []
            n = min(HT, NT - 1 - i)
            if n:
                e0 = block(NT - 1, i)
                found.append((0, 0, n, energy[:, e0:e0 + (NT + 2) * (n - 1) + 1:NT + 2, :], p_below[:, 0:n, :]))
            n = HT - 1 - i
            if n > 0:
                e0 = block(i + 1, i)
                found.append((1, slot(i + 1), n, energy[:, e0:e0 + (NT + 1) * (n - 1) + 1:NT + 1, :], p_right[:, i:HT - 1, :]))
            return found

        def left(i, h):
            js = sorted((j for j in range(i + 1) if slot(j) // HT == h), key=slot)
            return (slot(js[0]), js) if js else (0, [])

        def pt_events(i, h):
            return i + max(0, i - HT) + (i >= HT) + h

        x_dma = [sem("x_dma0"), sem("x_dma1")]
        x_stats = sem("x_stats")
        x_norm = sem("x_norm")
        xs_done = sem("xs_done")
        xh_done = sem("xh_done")
        xl_done = sem("xl_done")
        xt_t = sem("xt_t")
        xth_done = sem("xth_done")
        xtl_done = sem("xtl_done")
        e_ps = sem("e_ps")
        e_kept = sem("e_kept")
        a_dma = sem("a_dma")
        b_dma = sem("b_dma")
        w_dma = [sem("w_dma0"), sem("w_dma1")]
        a_masked = sem("a_masked")
        bt_t = sem("bt_t")
        bt_done = sem("bt_done")
        lora_ps = sem("lora_ps")
        weff_done = sem("weff_done")
        wt_t = sem("wt_t")
        wh_done = sem("wh_done")
        wl_done = sem("wl_done")
        cmin_done = sem("cmin_done")
        cmin_t = sem("cmin_t")
        rmin_t = sem("rmin_t")
        diff_done = sem("diff_done")
        eb_done = sem("eb_done")
        exp_done = sem("exp_done")
        expt_done = sem("expt_done")
        sum_t = sem("sum_t")
        pt_t = sem("pt_t")
        pth_done = sem("pth_done")
        ptl_done = sem("ptl_done")
        coef_done = sem("coef_done")
        pv_half = sem("pv_half")
        r_dma = [sem("r_dma0"), sem("r_dma1")]
        xs2_done = sem("xs2_done")
        att_evac = sem("att_evac")
        att_stats = sem("att_stats")
        att_norm = sem("att_norm")
        n_done = sem("n_done")
        x1_done = sem("x1_done")
        x1_stats = sem("x1_stats")
        x1_norm = sem("x1_norm")
        x2_done = sem("x2_done")
        x2t_t = sem("x2t_t")
        x2h_done = sem("x2h_done")
        x2l_done = sem("x2l_done")
        ffn_done = sem("ffn_done")
        y_evac = sem("y_evac")
        y_stats = sem("y_stats")
        y_norm = sem("y_norm")
        yn_done = sem("yn_done")
        out_ready = sem("out_ready")
        out_dma = sem("out_dma")
        bn_done = [sem(f"bn_done_{k}") for k in "xary"]
        veps_done = [sem(f"veps_done_{k}") for k in "xary"]
        r_done = [sem(f"r_done_{k}") for k in "xary"]
        emin_done = sem("emin_done")
        rmin_done = sem("rmin_done")
        rsum_done = sem("rsum_done")
        rinv_done = sem("rinv_done")
        const_dma = sem("const_dma")
        ident_zero = sem("ident_zero")
        const_ready = sem("const_ready")
        const_step = sem("const_step")
        bias_ready = sem("bias_ready")

        per_batch = {
            e_ps: ECHUNKS, e_kept: ECHUNKS, a_dma: DMA, a_masked: 1, bt_t: 1, bt_done: 1,
            lora_ps: 2 * NK, weff_done: 2 * NK, wt_t: 2 * NK, wh_done: 2 * NK, wl_done: 2 * NK,
            cmin_done: NT - 1, cmin_t: NT - 1, rmin_t: NT - 1, diff_done: NT - 1, expt_done: NT - 1, sum_t: NT - 1,
            emin_done: NT - 1, pt_t: pt_events(NT - 1, 1), pth_done: 2 * NT, ptl_done: 2 * NT, pv_half: 2 * NT,
            out_dma: DMA * NT,
        }
        for pair, n in ((x_dma, HT), (r_dma, HT), (w_dma, NK // 2)):
            per_batch.update({one: DMA * n for one in pair})
        primed = (y_evac, out_dma)

        XN, AN, RN, YN = range(4)

        def counts(b):
            def at(which, n):
                per = per_batch.get(which, NT)
                assert 0 <= n <= per, n
                return b * per + (n + 1 if which in primed else n)
            return at

        block_of = ctx.enter_context(nc.Block())

        @block_of.sync
        def _(sp):
            sp.sem_inc(out_dma, 1)

            def load_x(t, b, at):
                if t >= 2:
                    sp.wait_ge(xs_done, at(xs_done, t - 1))
                sp.dma_start(x_in[t % 2], x_tiles[bass.ds(b * NT + t, 1), :, :].rearrange("a p d -> (a p) d"))\
                  .then_inc(x_dma[t % 2], DMA)

            for t in range(HEAD):
                load_x(t, 0, counts(0))
            sp.dma_start(starts_i[:, :], starts.rearrange("(a n) -> a n", a=1).to_broadcast([KR, NSTART])).then_inc(const_dma, DMA)
            sp.dma_start(gamma_b[:, :], gamma.rearrange("(a n) -> a n", a=1).to_broadcast([P, 1])).then_inc(const_dma, DMA)
            sp.dma_start(bias_b[:, :], bias.rearrange("(a n) -> a n", a=1).to_broadcast([P, D])).then_inc(const_dma, DMA)
            for t in range(HEAD, HEAD + 2):
                load_x(t, 0, counts(0))
            for a in range(NA):
                sp.dma_start(b_raw[:, :, a * R:(a + 1) * R], lora_b[a].rearrange("(t p) r -> p t r", p=P)).then_inc(b_dma, DMA)
            with sp.Fori(0, NB) as b:
                at = counts(b)
                for t in range(HEAD + 2, NT):
                    load_x(t, b, at)
                sp.wait_ge(e_ps, at(e_ps, ECHUNKS))
                sp.dma_start(a_mat, lora_a.rearrange("a r d -> (a r) d")).then_inc(a_dma, DMA)

                def load_w(w):
                    if w >= 2:
                        sp.wait_ge(wt_t, at(wt_t, 2 * (w - 1)))
                    sp.dma_start(w_stage[w % 2], weight[w * P:(w + 1) * P, :]).then_inc(w_dma[w % 2], DMA)

                def load_row(i):
                    if i == 1:
                        sp.wait_ge(lora_ps, at(lora_ps, 2 * NK))
                    sp.dma_start(x1[:, i % 2, :], x_tiles[bass.ds(b * NT + i, 1), :, :].rearrange("a p d -> (a p) d"))\
                      .then_inc(r_dma[i % 2], DMA)

                def store(i):
                    sp.wait_ge(out_ready, at(out_ready, i + 1))
                    sp.dma_start(out_tiles[bass.ds(b * NT + i, 1), :, :].rearrange("a p d -> (a p) d"), y)\
                      .then_inc(out_dma, DMA)

                load_w(0)
                load_w(1)
                load_row(0)
                for w in range(2, NK):
                    load_w(w)
                load_row(1)
                for i in range(NT - 3):
                    store(i)
                    load_row(i + 2)
                with sp.If(b < LAST):
                    sp.wait_ge(pt_t, at(pt_t, pt_events(NT - 1, 1)))
                    for t in range(2):
                        load_x(t, LAST, counts(LAST))
                store(NT - 3)
                load_row(NT - 1)
                with sp.If(b < LAST):
                    for t in range(2, HEAD):
                        load_x(t, LAST, counts(LAST))
                store(NT - 2)
                with sp.If(b < LAST):
                    for t in range(HEAD, HEAD + 2):
                        load_x(t, LAST, counts(LAST))
                store(NT - 1)
            sp.wait_ge(out_dma, NB * per_batch[out_dma] + 1)

        @block_of.tensor
        def _(pe):
            pe.wait_ge(const_ready, 2)

            def product(ps, left, right, first, last):
                for n, (u, v) in enumerate(((0, 0), (0, 1), (1, 0))):
                    mm = nc.tensor.matmul(ps, left[u], right[v], start=first and n == 0, stop=last and n == 2)
                return mm

            def transpose_x(t, at):
                pe.wait_ge(xs_done, at(xs_done, t + 1))
                if t == HEAD:
                    pe.wait_ge(y_evac, at(y_evac, 0))
                elif t == 3:
                    pe.wait_ge(xtl_done, at(xtl_done, 1))
                elif t > HEAD:
                    pe.wait_ge(xtl_done, at(xtl_done, t - 1))
                for k in range(NK):
                    tr = nc.tensor.transpose(ps_xt[t][:, k * P:(k + 1) * P], xs[t % 2][:, k * P:(k + 1) * P], ident[:, :])
                tr.then_inc(xt_t, 1)

            for t in range(HEAD):
                transpose_x(t, counts(0))
            with pe.Fori(0, NB) as b:
                at = counts(b)
                done = 0

                def energy_chunk(j, c, beside=None):
                    nonlocal done
                    n = min(4, j + 1 - 4 * c)
                    if done >= 4:
                        pe.wait_ge(e_kept, at(e_kept, done - 3))
                    bank = ps_a[:, (done % 4) * BANK:(done % 4) * BANK + n * P]
                    for k in range(NK):
                        mm = product(bank, [xt[:, j, u, k, :] for u in range(2)],
                                     [xt[:, 4 * c:4 * c + n, u, k, :] for u in range(2)], k == 0, k == NK - 1)
                        if beside and k == 2:
                            beside(0)
                    mm.then_inc(e_ps, 1)
                    done += 1

                def energy_row(j):
                    pe.wait_ge(xtl_done, at(xtl_done, max(j, 2) + 1))
                    for c in range(chunks(j)):
                        energy_chunk(j, c)

                def transpose_b():
                    pe.wait_ge(b_dma, NA * DMA)
                    pe.wait_ge(rsum_done, at(rsum_done, 1))
                    pe.nop(nofuse=True)
                    for t in range(NK):
                        tr = nc.tensor.transpose(ps_c[0:KR, t * P:(t + 1) * P], b_raw[:, t, :], ident[:, :])
                    tr.then_inc(bt_t, 1)

                def lora(q):
                    w, h = q // 2, q % 2
                    if q == 0:
                        pe.wait_ge(bt_done, at(bt_done, 1))
                        pe.wait_ge(a_masked, at(a_masked, 1))
                    elif q > 1:
                        pe.wait_ge(wl_done, at(wl_done, q - 1))
                    nc.tensor.matmul(ps_c[:, h * BANK:(h + 1) * BANK], bt[:, w * P:(w + 1) * P],
                                     a_mat[:, h * BANK:(h + 1) * BANK], start=True, stop=True).then_inc(lora_ps, 1)

                def transpose_w(q):
                    w, h = q // 2, q % 2
                    pe.wait_ge(weff_done, at(weff_done, q + 1))
                    for k in range(h * HT // 2, (h + 1) * HT // 2):
                        tr = nc.tensor.transpose(ps_c[:, k * P:(k + 1) * P], w_stage[w % 2][:, k * P:(k + 1) * P], ident[:, :])
                    tr.then_inc(wt_t, 1)

                def due(products):
                    return min(max(products, 0) * (2 * NK + 1) // (2 * NT - 6), 2 * NK + 1)

                def prepare_weight(q):
                    if q:
                        transpose_w(q - 1)
                    if q < 2 * NK:
                        lora(q)

                def transpose_column_min(i):
                    if i == 0:
                        pe.wait_ge(cmin_done, at(cmin_done, 1))
                        pe.wait_ge(e_kept, at(e_kept, ECHUNKS - 3))
                        nc.tensor.transpose(ps_row(0, 2, 1), energy[:, block(NT - 1, 0), :], ident[:, :])
                    else:
                        pe.wait_ge(ptl_done, at(ptl_done, 2 * i))
                        if i == 1:
                            pe.wait_ge(e_kept, at(e_kept, ECHUNKS))
                        if i == NT - 1:
                            return
                        pe.wait_ge(cmin_done, at(cmin_done, i + 1))
                    for n, _ in enumerate(below(i)):
                        tr = nc.tensor.transpose(ps_row(i, n, 1), col_min[:, n, :], ident[:, :])
                    tr.then_inc(cmin_t, 1)

                def spread_row_min(i):
                    pe.wait_ge(rmin_done, at(rmin_done, i + 1))
                    nc.tensor.transpose(ps_row(i, 4, 1), rmin[:, i:i + 1].to_broadcast([P, P]), ident[:, :]).then_inc(rmin_t, 1)

                def transpose_p(i, h):
                    place, js = left(i, h)
                    if not js:
                        return
                    pe.wait_ge(exp_done, at(exp_done, i + 1))
                    if i < NT - 1:
                        pe.wait_ge(diff_done, at(diff_done, i + 1))
                    if h and i:
                        pe.wait_ge(rsum_done, at(rsum_done, i))
                    for n, j in enumerate(js):
                        tr = nc.tensor.transpose(ps_row(i, place + n, 1), energy[:, block(i, j), :], ident[:, :])
                    tr.then_inc(pt_t, 1)

                def sum_below(i):
                    if i == NT - 1:
                        return
                    pe.wait_ge(ptl_done, at(ptl_done, 2 * i + 2))
                    terms = [(q, u) for _, p0, n, _, _ in below(i) for q in range(p0, p0 + n) for u in range(2)]
                    for n, (q, u) in enumerate(terms):
                        mm = nc.tensor.matmul(ps_row(i, 12, 1)[:, 0:1], pt[:, u, q, :], ones[:, :], start=n == 0, stop=n == len(terms) - 1)
                    mm.then_inc(sum_t, 1)

                def attend(i, h):
                    pe.wait_ge(ptl_done, at(ptl_done, 2 * i + h + 1))
                    if h == 0:
                        if i:
                            pe.wait_ge(att_evac, at(att_evac, i))
                        else:
                            pe.wait_ge(xl_done, at(xl_done, NT))
                    for q in range(h * HT, (h + 1) * HT):
                        j = NT - 1 - q if q < HT else q - HT
                        for c in range(2):
                            mm = product(ps_b[:, c * BANK:(c + 1) * BANK], [pt[:, u, q, :] for u in range(2)],
                                         [z[:, j, c * BANK:(c + 1) * BANK] for z in (x_high, x_low)], q == 0, q == NT - 1)
                            done = 2 * (q - 2) + c
                            if i == 0 and due(done) < due(done + 1):
                                prepare_weight(due(done))
                        if q == (h + 1) * HT - 1:
                            mm.then_inc(pv_half, 1)
                        if i and q == 1:
                            sum_below(i)
                            if i + 1 < NT:
                                transpose_column_min(i + 1)
                        if q == (3 if i else 2) and i + 1 < NT - 1:
                            spread_row_min(i + 1)
                        if i == 0 and q == 0:
                            transpose_b()

                def transpose_x2(i):
                    pe.wait_ge(x2_done, at(x2_done, i + 1))
                    if i:
                        pe.wait_ge(y_evac, at(y_evac, i))
                    else:
                        pe.wait_ge(wl_done, at(wl_done, 2 * NK))
                    for k in range(NK):
                        tr = nc.tensor.transpose(ps_c[:, k * P:(k + 1) * P], att[:, k * P:(k + 1) * P], ident[:, :])
                    tr.then_inc(x2t_t, 1)

                def feed_forward(i):
                    pe.wait_ge(x2l_done, at(x2l_done, i + 1))
                    for c in range(2):
                        for k in range(NK):
                            mm = product(ps_c[:, c * BANK:(c + 1) * BANK], [x2t[:, u, k, :] for u in range(2)],
                                         [wt[:, u, k, c * BANK:(c + 1) * BANK] for u in range(2)], k == 0, k == NK - 1)
                    mm.then_inc(ffn_done, 1)

                for kind, n in order[:-1]:
                    if kind == "T":
                        transpose_x(n, at)
                    else:
                        energy_row(n)
                pe.wait_ge(xtl_done, at(xtl_done, NT))
                energy_chunk(NT - 1, 0)
                energy_chunk(NT - 1, 1)
                transpose_column_min(0)
                energy_chunk(NT - 1, 2, beside=spread_row_min)
                transpose_p(0, 1)
                energy_chunk(NT - 1, 3)
                for i in range(NT):
                    if i == 0:
                        sum_below(0)
                        transpose_column_min(1)
                    attend(i, 0)
                    if i + 1 < NT:
                        transpose_p(i + 1, 0)
                    if i:
                        transpose_x2(i - 1)
                    attend(i, 1)
                    if i + 1 < NT:
                        transpose_p(i + 1, 1)
                    if i:
                        feed_forward(i - 1)
                with pe.If(b < LAST):
                    pe.wait_ge(att_evac, at(att_evac, NT))
                    transpose_x(0, counts(LAST))
                    transpose_x(1, counts(LAST))
                transpose_x2(NT - 1)
                with pe.If(b < LAST):
                    transpose_x(2, counts(LAST))
                feed_forward(NT - 1)
                with pe.If(b < LAST):
                    transpose_x(3, counts(LAST))

        @block_of.vector
        def _(dve):
            dve.sem_inc(y_evac, 1)

            def row_stats(kind, n, rows, done, at):
                nc.vector.bn_stats(bn[:, kind, 0, :], rows[:, 0:BANK])
                nc.vector.bn_stats(bn[:, kind, 1, :], rows[:, BANK:D]).then_inc(bn_done[kind], 1)
                dve.wait_ge(bn_done[kind], at(bn_done[kind], n + 1))
                dve.nop(nofuse=True)
                nc.vector.bn_aggr(mv[:, kind, :], bn[:, kind, :, :]).then_inc(done, 1)

            def stats_x(t, at):
                dve.wait_ge(x_dma[t % 2], at(x_dma[t % 2], DMA * (t // 2 + 1)))
                if t:
                    dve.wait_ge(x_norm, at(x_norm, t))
                row_stats(XN, t, x_in[t % 2], x_stats, at)

            def split_xt(t, at):
                dve.wait_ge(xth_done, at(xth_done, t + 1))
                nc.vector.tensor_tensor(xt[:, t, 1, :, :].rearrange("p k n -> p (k n)"), ps_xt[t][:, :],
                                        xt[:, t, 0, :, :].rearrange("p k n -> p (k n)"), ALU.subtract).then_inc(xtl_done, 1)

            stats_x(0, counts(0))
            for t in range(HEAD):
                if t + 1 < HEAD:
                    stats_x(t + 1, counts(0))
                if t:
                    split_xt(t - 1, counts(0))
            stats_x(HEAD, counts(0))
            split_xt(HEAD - 1, counts(0))

            count = [0]

            dve.wait_ge(const_dma, 3 * DMA)
            dve.wait_ge(const_ready, 2)

            def const(ins):
                count[0] += 1
                ins.then_inc(const_step, 1)
                dve.wait_ge(const_step, count[0])

            const(nc.vector.tensor_copy(starts_f[:, :], starts_i[:, :]))
            for n in range(NB):
                lo, hi = is_below[:, n, :], seg[:, n, :]
                const(nc.vector.tensor_scalar(lo, starts_f[:, :], float(n), None, ALU.is_le))
                const(nc.vector.tensor_scalar(hi[:, 0:1], lo[:, 0:1], -1.0, 2.0, ALU.mult, ALU.add))
                const(nc.vector.scalar_tensor_tensor(hi[:, 1:2], hi[:, 0:1], lo[:, 1:2], lo[:, 0:1], ALU.mult, ALU.add))
                const(nc.vector.scalar_tensor_tensor(hi[:, 2:3], lo[:, 3:4], 3.0, hi[:, 1:2], ALU.add, ALU.subtract))
                const(nc.vector.scalar_tensor_tensor(hi[:, 3:4], hi[:, 2:3], lo[:, 2:3], hi[:, 1:2], ALU.mult, ALU.add))
                const(nc.vector.scalar_tensor_tensor(hi[:, 0:1], hi[:, 3:4], -float(R), row_id[:, :], ALU.mult, ALU.add))
                const(nc.vector.tensor_scalar(hi[:, 1:2], hi[:, 0:1], -2.0 * R, None, ALU.is_ge))
                const(nc.vector.scalar_tensor_tensor(mask[:, n:n + 1], hi[:, 0:1], float(-R), hi[:, 1:2], ALU.is_lt, ALU.mult))
            nc.vector.tensor_scalar(bias_b[:, :], bias_b[:, :], XS * WS, None, ALU.mult).then_inc(bias_ready, 1)
            dve.wait_ge(bias_ready, 1)

            with dve.Fori(0, NB) as b:
                at = counts(b)
                done = 0

                def keep_chunk(j, c):
                    nonlocal done
                    n = min(4, j + 1 - 4 * c)
                    dve.wait_ge(e_ps, at(e_ps, done + 1))
                    place = block(j, 4 * c)
                    nc.vector.tensor_scalar(flat[:, place * P:(place + n) * P], ps_a[:, (done % 4) * BANK:(done % 4) * BANK + n * P],
                                            1.0, None, ALU.mult, ALU.min, accum_out=emin[:, j, c:c + 1]).then_inc(e_kept, 1)
                    done += 1

                def keep_energy(j):
                    if j >= NT - 3:
                        dve.wait_ge(xt_t, at(xt_t, NT))
                        dve.wait_ge(xl_done, at(xl_done, NT))
                    for c in range(chunks(j)):
                        keep_chunk(j, c)

                stats_x(HEAD + 1, at)
                for kind, n in order[:-1]:
                    if kind == "T":
                        split_xt(n, at)
                        if n + 2 < NT:
                            stats_x(n + 2, at)
                    else:
                        keep_energy(n)
                dve.wait_ge(e_kept, at(e_kept, ECHUNKS - 4))

                def column_minimum(i, pieces=(0, 1)):
                    if i >= NT - 1:
                        return
                    for n, (_, _, _, e, _) in enumerate(below(i)):
                        if n not in pieces:
                            continue
                        if i == 0 and n == 0:
                            e = e[:, 1:HT, :]
                        m = nc.vector.tensor_reduce(col_min[:, n, :], e.rearrange("p j n -> p n j"), AX.X, ALU.min)
                    if len(below(i)) - 1 in pieces:
                        m.then_inc(cmin_done, 1)

                def row_minimum(i):
                    parts = chunks(i)
                    if i < NT - 1:
                        dve.wait_ge(cmin_t, at(cmin_t, i + 1))
                        nc.vector.tensor_reduce(emin[:, i, parts:parts + 1], ps_row(i, 0, len(below(i)) + (i == 0)), AX.X, ALU.min)\
                          .then_inc(emin_done, 1)
                        parts += 1
                        dve.wait_ge(emin_done, at(emin_done, i + 1))
                    else:
                        dve.wait_ge(e_kept, at(e_kept, ECHUNKS))
                    nc.vector.tensor_reduce(rmin[:, i:i + 1], emin[:, i, 0:parts], AX.X, ALU.min).then_inc(rmin_done, 1)
                    dve.wait_ge(rmin_done, at(rmin_done, i + 1))
                    nc.vector.tensor_scalar(ebias[:, i:i + 1], rmin[:, i:i + 1], 1.0 / (XS * XS), LN14, ALU.mult, ALU.add)\
                      .then_inc(eb_done, 1)

                def less_minimum(i, pieces=(0, 1)):
                    if i == NT - 1:
                        return
                    dve.wait_ge(rmin_t, at(rmin_t, i + 1))
                    for half, (_, _, n, e, p) in enumerate(below(i)):
                        if half not in pieces:
                            continue
                        m = nc.vector.tensor_tensor(p, e, ps_row(i, 4, 1).rearrange("p (j n) -> p j n", j=1).to_broadcast([P, n, P]),
                                                    ALU.subtract)
                    if len(below(i)) - 1 in pieces:
                        m.then_inc(diff_done, 1)

                def coefficient(i):
                    dve.wait_ge(exp_done, at(exp_done, i + 1))
                    if i < NT - 1:
                        dve.wait_ge(sum_t, at(sum_t, i + 1))
                        nc.vector.tensor_tensor(rsum[:, i % 2:i % 2 + 1], ps_row(i, 12, 1)[:, 0:1], esum[:, i:i + 1], ALU.add).then_inc(rsum_done, 1)
                    else:
                        nc.vector.tensor_copy(rsum[:, i % 2:i % 2 + 1], esum[:, i:i + 1]).then_inc(rsum_done, 1)
                    dve.wait_ge(rsum_done, at(rsum_done, i + 1))
                    nc.vector.reciprocal(rinv[:, i % 2:i % 2 + 1], rsum[:, i % 2:i % 2 + 1]).then_inc(rinv_done, 1)
                    dve.wait_ge(rinv_done, at(rinv_done, i + 1))
                    nc.vector.tensor_tensor(coef[:, i % 2:i % 2 + 1], rinv[:, i % 2:i % 2 + 1], gamma_b[:, :], ALU.mult).then_inc(coef_done, 1)

                def split_pt(i, h):
                    dve.wait_ge(pth_done, at(pth_done, 2 * i + h + 1))
                    place, js = left(i, h)
                    parts = [(place, len(js), ps_row(i, place, len(js)).rearrange("p (j n) -> p j n", n=P))] if js else []
                    parts += [(p0, n, p) for half, p0, n, _, p in below(i) if half == h]
                    for p0, n, source in parts:
                        low = nc.vector.tensor_tensor(pt[:, 1, p0:p0 + n, :], source, pt[:, 0, p0:p0 + n, :], ALU.subtract)
                    low.then_inc(ptl_done, 1)

                def mask_adapters():
                    dve.wait_ge(bt_t, at(bt_t, 1))
                    nc.vector.tensor_copy(bt, ps_c[0:KR, :]).then_inc(bt_done, 1)
                    dve.wait_ge(a_dma, at(a_dma, DMA))
                    nc.vector.tensor_scalar(a_mat, a_mat, mask[:, bass.ds(b, 1)], None, ALU.mult).then_inc(a_masked, 1)

                def add_adapter(q):
                    w, h = q // 2, q % 2
                    dve.wait_ge(w_dma[w % 2], at(w_dma[w % 2], DMA * (w // 2 + 1)))
                    dve.wait_ge(lora_ps, at(lora_ps, q + 1))
                    half = w_stage[w % 2][:, h * BANK:(h + 1) * BANK]
                    nc.vector.tensor_tensor(half, ps_c[:, h * BANK:(h + 1) * BANK], half, ALU.add).then_inc(weff_done, 1)

                def split_weight(q):
                    w, k = q // 2, q % 2 * (NK // 2)
                    dve.wait_ge(wh_done, at(wh_done, q + 1))
                    nc.vector.scalar_tensor_tensor(wt[:, 1, k:k + NK // 2, w * P:(w + 1) * P],
                                                   ps_c[:, k * P:k * P + BANK].rearrange("p (k n) -> p k n", k=NK // 2), WS,
                                                   wt[:, 0, k:k + NK // 2, w * P:(w + 1) * P], ALU.mult, ALU.subtract).then_inc(wl_done, 1)

                def prepare_weight(first, end):
                    for q in range(first, end):
                        if q < 2 * NK:
                            add_adapter(q)
                        if q:
                            split_weight(q - 1)

                def attended(i):
                    dve.wait_ge(pv_half, at(pv_half, 2 * i + 2))
                    dve.wait_ge(xs2_done, at(xs2_done, i + 1))
                    dve.wait_ge(coef_done, at(coef_done, i + 1))
                    nc.vector.scalar_tensor_tensor(att, ps_b[:, :], coef[:, i % 2:i % 2 + 1], att, ALU.mult, ALU.add)\
                      .then_inc(att_evac, 1)
                    dve.wait_ge(att_evac, at(att_evac, i + 1))
                    if i:
                        dve.wait_ge(att_norm, at(att_norm, i))
                    row_stats(AN, i, att, att_stats, at)

                def stats_x1(i):
                    dve.wait_ge(x1_done, at(x1_done, i + 1))
                    if i:
                        dve.wait_ge(x1_norm, at(x1_norm, i))
                    row_stats(RN, i, x1[:, i % 2, :], x1_stats, at)

                def split_x2(i):
                    dve.wait_ge(x2h_done, at(x2h_done, i + 1))
                    nc.vector.tensor_tensor(x2t[:, 1, :, :].rearrange("p k n -> p (k n)"), ps_c[:, :],
                                            x2t[:, 0, :, :].rearrange("p k n -> p (k n)"), ALU.subtract).then_inc(x2l_done, 1)

                def stats_y(i):
                    dve.wait_ge(ffn_done, at(ffn_done, i + 1))
                    if i:
                        dve.wait_ge(out_dma, at(out_dma, DMA * i))
                        dve.wait_ge(y_norm, at(y_norm, i))
                    nc.vector.tensor_tensor(y, ps_c[:, :], bias_b[:, :], ALU.add).then_inc(y_evac, 1)
                    dve.wait_ge(y_evac, at(y_evac, i + 1))
                    row_stats(YN, i, y, y_stats, at)

                column_minimum(0)
                keep_chunk(NT - 1, 0)
                keep_chunk(NT - 1, 1)
                row_minimum(0)
                column_minimum(1)
                less_minimum(0)
                keep_chunk(NT - 1, 2)
                split_pt(0, 0)
                split_pt(0, 1)
                keep_chunk(NT - 1, 3)
                coefficient(0)
                mask_adapters()
                for i in range(NT - 1):
                    row_minimum(i + 1)
                    if i:
                        coefficient(i)
                    if i >= 2:
                        stats_y(i - 2)
                    if i == 1:
                        stats_x1(0)
                    if i:
                        less_minimum(i + 1)
                        column_minimum(i + 2)
                    else:
                        for n in range(2):
                            prepare_weight(n, n + 1)
                            less_minimum(1, [n])
                        for n in range(2):
                            prepare_weight(n + 2, n + 3)
                            column_minimum(2, [n])
                        prepare_weight(4, HT - 1)
                    split_pt(i + 1, 0)
                    if i:
                        split_x2(i - 1)
                    else:
                        prepare_weight(HT - 1, 2 * NK + 1)
                    attended(i)
                    split_pt(i + 1, 1)
                    if i:
                        stats_x1(i)
                stats_y(NT - 3)
                split_x2(NT - 2)
                coefficient(NT - 1)
                with dve.If(b < LAST):
                    stats_x(0, counts(LAST))
                    stats_x(1, counts(LAST))
                attended(NT - 1)
                with dve.If(b < LAST):
                    stats_x(2, counts(LAST))
                stats_x1(NT - 1)
                stats_y(NT - 2)
                with dve.If(b < LAST):
                    split_xt(0, counts(LAST))
                    stats_x(3, counts(LAST))
                split_x2(NT - 1)
                with dve.If(b < LAST):
                    split_xt(1, counts(LAST))
                    split_xt(2, counts(LAST))
                    stats_x(4, counts(LAST))
                stats_y(NT - 1)
                with dve.If(b < LAST):
                    split_xt(3, counts(LAST))

        @block_of.scalar
        def _(act):
            def norm_x(t, at):
                act.wait_ge(x_norm, at(x_norm, t + 1))
                if t >= 2:
                    act.wait_ge(xt_t, at(xt_t, t - 1))
                    act.wait_ge(xl_done, at(xl_done, t - 1))
                nc.scalar.activation(xs[t % 2], x_in[t % 2], ACT.Identity, bias=x_nb[:, t:t + 1], scale=x_r[:, t:t + 1])\
                  .then_inc(xs_done, 1)

            def high_x(t, at):
                act.wait_ge(xs_done, at(xs_done, t + 1))
                nc.scalar.activation(x_high[:, t, :], xs[t % 2], ACT.Copy).then_inc(xh_done, 1)

            def split_xt(t, at):
                act.wait_ge(xt_t, at(xt_t, t + 1))
                if t == NT - 3:
                    act.wait_ge(out_dma, at(out_dma, 0))
                nc.scalar.activation(xt[:, t, 0, :, :].rearrange("p k n -> p (k n)"), ps_xt[t][:, :], ACT.Copy)\
                  .then_inc(xth_done, 1)

            act.wait_ge(const_ready, 2)
            norm_x(0, counts(0))
            for t in range(HEAD):
                high_x(t, counts(0))
                if t + 1 < HEAD:
                    norm_x(t + 1, counts(0))
                split_xt(t, counts(0))
            norm_x(HEAD, counts(0))
            high_x(HEAD, counts(0))
            with act.Fori(0, NB) as b:
                at = counts(b)
                for kind, t in order:
                    if kind == "T":
                        split_xt(t, at)
                        if t + 1 < NT:
                            norm_x(t + 1, at)
                            high_x(t + 1, at)

                def exponentials(i):
                    act.wait_ge(eb_done, at(eb_done, i + 1))
                    row = flat[:, block(i, 0) * P:(block(i, 0) + i + 1) * P]
                    nc.scalar.activation(row, row, ACT.Exp, bias=ebias[:, i:i + 1], scale=-1.0 / (XS * XS),
                                         accum_out=esum[:, i:i + 1]).then_inc(exp_done, 1)

                def exponentials_below(i):
                    if i == NT - 1:
                        return
                    act.wait_ge(diff_done, at(diff_done, i + 1))
                    for _, _, _, _, p in below(i):
                        e = nc.scalar.activation(p, p, ACT.Exp, bias=ln14[:, 0:1], scale=-1.0 / (XS * XS))
                    e.then_inc(expt_done, 1)

                def split_pt(i, h):
                    place, js = left(i, h)
                    parts = []
                    if js:
                        act.wait_ge(pt_t, at(pt_t, pt_events(i, h)))
                        parts.append((place, len(js), ps_row(i, place, len(js)).rearrange("p (j n) -> p j n", n=P)))
                    if i < NT - 1:
                        act.wait_ge(expt_done, at(expt_done, i + 1))
                    if i:
                        act.wait_ge(pv_half, at(pv_half, 2 * i - 1 + h))
                    parts += [(p0, n, p) for half, p0, n, _, p in below(i) if half == h]
                    for p0, n, source in parts:
                        high = nc.scalar.activation(pt[:, 0, p0:p0 + n, :], source, ACT.Copy)
                    high.then_inc(pth_done, 1)

                def high_weight(first, end):
                    for q in range(first, end):
                        w, k = q // 2, q % 2 * (NK // 2)
                        act.wait_ge(wt_t, at(wt_t, q + 1))
                        if q == 0:
                            act.wait_ge(e_ps, at(e_ps, ECHUNKS))
                        nc.scalar.activation(wt[:, 0, k:k + NK // 2, w * P:(w + 1) * P],
                                             ps_c[:, k * P:k * P + BANK].rearrange("p (k n) -> p k n", k=NK // 2), ACT.Copy,
                                             scale=WS).then_inc(wh_done, 1)

                def norm_rows(i):
                    act.wait_ge(r_dma[i % 2], at(r_dma[i % 2], DMA * (i // 2 + 1)))
                    if i:
                        act.wait_ge(x2t_t, at(x2t_t, i))
                    else:
                        act.wait_ge(lora_ps, at(lora_ps, 2 * NK))
                    nc.scalar.activation(att, x1[:, i % 2, :], ACT.Identity, bias=x_nb[:, i:i + 1], scale=x_r[:, i:i + 1])\
                      .then_inc(xs2_done, 1)

                def split_x2(i):
                    act.wait_ge(x2t_t, at(x2t_t, i + 1))
                    if i:
                        act.wait_ge(ffn_done, at(ffn_done, i))
                    else:
                        act.wait_ge(wt_t, at(wt_t, 2 * NK))
                    nc.scalar.activation(x2t[:, 0, :, :].rearrange("p k n -> p (k n)"), ps_c[:, :], ACT.Copy).then_inc(x2h_done, 1)

                def norm_attended(i):
                    act.wait_ge(att_norm, at(att_norm, i + 1))
                    nc.scalar.activation(att, att, ACT.Identity, bias=ln_nb[:, 0:1], scale=ln_r[:, 0:1]).then_inc(n_done, 1)

                def norm_x1(i):
                    act.wait_ge(x1_norm, at(x1_norm, i + 1))
                    nc.scalar.activation(att, x1[:, i % 2, :], ACT.Identity, bias=ln_nb[:, 1:2], scale=ln_r[:, 1:2])\
                      .then_inc(x2_done, 1)

                def norm_y(i):
                    act.wait_ge(y_norm, at(y_norm, i + 1))
                    nc.scalar.activation(y, y, ACT.Identity, bias=ln_nb[:, 2:3], scale=ln_r[:, 2:3]).then_inc(yn_done, 1)

                exponentials(0)
                exponentials_below(0)
                split_pt(0, 0)
                split_pt(0, 1)
                for i in range(NT - 1):
                    exponentials(i + 1)
                    if i == 1:
                        norm_x1(0)
                    if i >= 2:
                        norm_y(i - 2)
                    if i == 0:
                        high_weight(0, 2)
                    exponentials_below(i + 1)
                    if i == 0:
                        high_weight(2, HT - 2)
                    split_pt(i + 1, 0)
                    if i:
                        split_x2(i - 1)
                    else:
                        high_weight(HT - 2, 2 * NK - 1)
                    norm_rows(i)
                    if i == 0:
                        high_weight(2 * NK - 1, 2 * NK)
                    split_pt(i + 1, 1)
                    norm_attended(i)
                    if i:
                        norm_x1(i)
                norm_y(NT - 3)
                split_x2(NT - 2)
                norm_rows(NT - 1)
                with act.If(b < LAST):
                    norm_x(0, counts(LAST))
                    norm_x(1, counts(LAST))
                norm_attended(NT - 1)
                with act.If(b < LAST):
                    act.wait_ge(pv_half, at(pv_half, 2 * NT))
                    high_x(0, counts(LAST))
                norm_x1(NT - 1)
                with act.If(b < LAST):
                    high_x(1, counts(LAST))
                    split_xt(0, counts(LAST))
                    norm_x(2, counts(LAST))
                split_x2(NT - 1)
                norm_y(NT - 2)
                with act.If(b < LAST):
                    split_xt(1, counts(LAST))
                    high_x(2, counts(LAST))
                    norm_x(3, counts(LAST))
                    split_xt(2, counts(LAST))
                    high_x(3, counts(LAST))
                    norm_x(4, counts(LAST))
                    split_xt(3, counts(LAST))
                    high_x(4, counts(LAST))
                norm_y(NT - 1)

        @block_of.gpsimd
        def _(pool):
            nc.gpsimd.memset(ident[:, :], 0.0).then_inc(ident_zero, 1)
            nc.gpsimd.memset(neg_half[:, :], -0.5)
            nc.gpsimd.memset(ones[:, :], 1.0)
            nc.gpsimd.memset(ln14[:, :], LN14)
            nc.gpsimd.iota(row_id[:, :], [[0, 1]], base=0, channel_multiplier=1, allow_small_or_imprecise_dtypes=True).then_inc(const_ready, 1)
            pool.wait_ge(ident_zero, 1)
            nc.gpsimd.affine_select(out=ident[:, :], in_=ident[:, :], compare_op=ALU.not_equal, fill=1.0,
                                    base=0, pattern=[[-1, P]], channel_multiplier=1).then_inc(const_ready, 1)
            pool.wait_ge(const_ready, 2)

            def norm(kind, n, scale, eps, r, nb, done, at):
                pool.nop(nofuse=True)
                nc.gpsimd.tensor_scalar(veps[:, kind:kind + 1], mv[:, kind, 1:2], scale, eps, ALU.mult, ALU.add)\
                  .then_inc(veps_done[kind], 1)
                pool.wait_ge(veps_done[kind], at(veps_done[kind], n + 1))
                nc.gpsimd.tensor_tensor(r, veps[:, kind:kind + 1], neg_half[:, :], ALU.pow).then_inc(r_done[kind], 1)
                pool.wait_ge(r_done[kind], at(r_done[kind], n + 1))
                pool.nop(nofuse=True)
                nc.gpsimd.tensor_scalar(nb, mv[:, kind, 0:1], r, -1.0, ALU.mult, ALU.mult).then_inc(done, 1)

            def norm_x(t, at):
                pool.wait_ge(x_stats, at(x_stats, t + 1))
                norm(XN, t, XS ** -2, EPS * XS ** -2, x_r[:, t:t + 1], x_nb[:, t:t + 1], x_norm, at)

            def low_x(t, at):
                pool.wait_ge(xh_done, at(xh_done, t + 1))
                nc.gpsimd.tensor_tensor(x_low[:, t, :], xs[t % 2], x_high[:, t, :], ALU.subtract).then_inc(xl_done, 1)

            norm_x(0, counts(0))
            norm_x(1, counts(0))
            for t in range(HEAD):
                low_x(t, counts(0))
                if t + 2 <= HEAD:
                    norm_x(t + 2, counts(0))
            with pool.Fori(0, NB) as b:
                at = counts(b)
                norm_x(HEAD + 1, at)
                for t in range(HEAD, NT):
                    low_x(t, at)
                    if t + 2 < NT:
                        norm_x(t + 2, at)

                def finish_y(i):
                    pool.wait_ge(y_stats, at(y_stats, i + 1))
                    norm(YN, i, 1.0, EPS * (XS * WS) ** 2, ln_r[:, 2:3], ln_nb[:, 2:3], y_norm, at)
                    pool.wait_ge(yn_done, at(yn_done, i + 1))
                    nc.gpsimd.tensor_tensor(y, x1[:, i % 2, :], y, ALU.add).then_inc(out_ready, 1)

                def residual(i):
                    pool.wait_ge(att_stats, at(att_stats, i + 1))
                    norm(AN, i, 1.0, EPS * XS ** 2, ln_r[:, 0:1], ln_nb[:, 0:1], att_norm, at)
                    pool.wait_ge(n_done, at(n_done, i + 1))
                    nc.gpsimd.tensor_tensor(x1[:, i % 2, :], x1[:, i % 2, :], att, ALU.add).then_inc(x1_done, 1)

                def norm_residual(i):
                    pool.wait_ge(x1_stats, at(x1_stats, i + 1))
                    norm(RN, i, XS ** -2, EPS * XS ** -2, ln_r[:, 1:2], ln_nb[:, 1:2], x1_norm, at)

                for i in range(NT - 1):
                    if i >= 2:
                        finish_y(i - 2)
                    residual(i)
                    norm_residual(i)
                finish_y(NT - 3)
                with pool.If(b < LAST):
                    norm_x(0, counts(LAST))
                    norm_x(1, counts(LAST))
                residual(NT - 1)
                with pool.If(b < LAST):
                    norm_x(2, counts(LAST))
                norm_residual(NT - 1)
                with pool.If(b < LAST):
                    low_x(0, counts(LAST))
                    low_x(1, counts(LAST))
                    norm_x(3, counts(LAST))
                finish_y(NT - 2)
                with pool.If(b < LAST):
                    low_x(2, counts(LAST))
                    low_x(3, counts(LAST))
                    norm_x(4, counts(LAST))
                finish_y(NT - 1)


_INS = ["L0_attn_x", "L0_attn_gamma", "L0_ffn_weight", "L0_ffn_bias", "L0_ffn_lora_A", "L0_ffn_lora_B",
        "L0_ffn_lora_start_indices"]


def kernel(**inputs):
    import numpy as np
    import concourse.bacc as bacc
    from concourse.bass_utils import run_bass_kernel_spmd

    nc = bacc.Bacc("TRN2", target_bir_lowering=False, num_devices=1)
    arrays, args = {}, []
    for name in _INS:
        a = np.ascontiguousarray(inputs[name])
        arrays[f"in_{name}"] = a
        args.append(nc.dram_tensor(f"in_{name}", a.shape, mybir.dt.from_np(a.dtype), kind="ExternalInput").ap())
    shape = inputs["L0_attn_x"].shape
    args.append(nc.dram_tensor("out_x", shape, F32, kind="ExternalOutput").ap())
    sandwich(nc, *args)
    r = run_bass_kernel_spmd(nc, [arrays], core_ids=[0])
    return r.results[0]["out_x"]
```

```python
from contextlib import ExitStack

import concourse.bass as bass
from concourse import mybir

ALU = mybir.AluOpType
ACT = mybir.ActivationFunctionType
AX = mybir.AxisListType
F32 = mybir.dt.float32
F16 = mybir.dt.float16
I32 = mybir.dt.int32

P = 128
BANK = 512
EPS = 1e-5
LN14 = 9.704060527839234
XS = 1024.0
WS = 64.0
LS = 64.0
DMA = 16


def sandwich(nc, x, gamma, weight, bias, lora_a, lora_b, starts, out):
    NB, S, D = x.shape
    NA, R, _ = lora_a.shape
    NT = S // P
    NK = D // P
    HT = NT // 2
    KR = NA * R
    NSTART = starts.shape[0]
    LAST = NB - 1
    assert NB == 2 and D == 2 * BANK and weight.shape[0] == D and NT == 16 and NSTART == 4 and NA == 3

    def chunks(j):
        return -(-(j + 1) // 4)

    def chunk_number(j, c):
        return sum(chunks(r) for r in range(j)) + c

    ECHUNKS = chunk_number(NT, 0)

    HEAD = 4
    order = [("T", HEAD)]
    for j in range(HEAD - 1, NT):
        order.append(("E", j))
        if j + 2 < NT:
            order.append(("T", j + 2))

    x_tiles = x.rearrange("b (t p) d -> (b t) p d", p=P)
    out_tiles = out.rearrange("b (t p) d -> (b t) p d", p=P)

    with ExitStack() as ctx:
        def sb(name, shape, dt):
            return ctx.enter_context(nc.sbuf_tensor(name, shape, dt))

        def sem(name):
            return ctx.enter_context(nc.semaphore(name))

        energy = sb("energy", [P, HT * (NT + 1), P], F32)
        x_high = sb("x_high", [P, NT, D], F16)
        x_low = sb("x_low", [P, NT, D], F16)
        region = sb("region", [P, NT * 2 * NK * P], F16)
        xt = region[:, :].rearrange("p (t s k n) -> p t s k n", t=NT, s=2, k=NK)
        TILE = 2 * NK * P

        def part(tile, n, dt):
            a = region[:, tile * TILE:(tile + n) * TILE]
            return a if dt == F16 else a.bitcast(dt)

        pt = part(1, 2, F16).rearrange("p (s j n) -> p s j n", s=2, j=NT)
        x1 = part(14, 2, F32).rearrange("p (r n) -> p r n", r=2)
        att = part(3, 1, F32)
        x2t = part(12, 1, F16).rearrange("p (s k n) -> p s k n", s=2, k=NK)
        y = part(13, 1, F32)
        p_below = part(0, 1, F32).rearrange("p (j n) -> p j n", n=P)
        wt = part(4, 8, F16).rearrange("p (s k n) -> p s k n", s=2, k=NK)
        w_stage = [part(13, 1, F32), part(12, 1, F32)]
        bt = part(3, 1, F16)[0:KR, :].rearrange("r (s n) -> r s n", s=2)
        a_mat = x1[0:KR, 1, :]
        a_split = wt[0:KR, :, :, (NK - 1) * P:NK * P]
        flat = energy[:, :, :].rearrange("p b n -> p (b n)")
        x_in = [flat[:, P:P + D], flat[:, P + D:P + 2 * D]]
        xs = [flat[:, (2 * (NT + 1) + 3) * P:(2 * (NT + 1) + 3) * P + D],
              flat[:, (NT + 1 + 2) * P:(NT + 1 + 2) * P + D]]
        x_first = x_in + [flat[:, n * (NT + 1) * P:n * (NT + 1) * P + D] for n in (HT - 2, HT - 1)]

        p_right = sb("p_right", [P, HT - 1, P], F32)
        b_raw = sb("b_raw", [P, NK, KR], F32)
        col_min = sb("col_min", [P, 2, P], F32)
        ones = sb("ones", [P, 1], F32)
        ln14 = sb("ln14", [P, 1], F32)
        ident = sb("ident", [P, P], F32)
        bias_b = sb("bias_b", [P, D], F32)
        gamma_b = sb("gamma_b", [P, 1], F32)
        neg_half = sb("neg_half", [P, 1], F32)
        starts_i = sb("starts_i", [KR, NSTART], I32)
        starts_f = sb("starts_f", [KR, NSTART], F32)
        row_id = sb("row_id", [KR, 1], F32)
        is_below = sb("is_below", [KR, NB, NSTART], F32)
        seg = sb("seg", [KR, NB, 4], F32)
        mask = sb("mask", [KR, NB], F32)
        bn = sb("bn", [P, 4, 2, 6], F32)
        mv = sb("mv", [P, 4, 2], F32)
        veps = sb("veps", [P, 4], F32)
        x_r = sb("x_r", [P, NT], F32)
        x_nb = sb("x_nb", [P, NT], F32)
        ln_r = sb("ln_r", [P, 3], F32)
        ln_nb = sb("ln_nb", [P, 3], F32)
        emin = sb("emin", [P, NT, 5], F32)
        rmin = sb("rmin", [P, NT], F32)
        ebias = sb("ebias", [P, NT], F32)
        esum = sb("esum", [P, NT], F32)
        rsum = sb("rsum", [P, 2], F32)
        rinv = sb("rinv", [P, 2], F32)
        coef = sb("coef", [P, 2], F32)

        ps_a = ctx.enter_context(nc.psum_tensor("ps_a", [P, 4 * BANK], F32))
        ps_b = ctx.enter_context(nc.psum_tensor("ps_b", [P, 2 * BANK], F32))
        ps_c = ctx.enter_context(nc.psum_tensor("ps_c", [P, 2 * BANK], F32))
        def ps_row(i, place, n):
            if i:
                return ps_a[:, place * P:(place + n) * P]
            return (ps_b if place < HT else ps_c)[:, place % HT * P:(place % HT + n) * P]

        ps_xt = [ps_b, ps_a[:, 2 * BANK:4 * BANK]] * 2 + [(ps_c, ps_b)[t % 2] for t in range(HEAD, NT)]

        def block(j, i):
            return j * (NT + 1) + i if j < HT else (NT - 1 - j) * (NT + 1) + NT - j + i

        def slot(j):
            return NT - 1 - j if j >= HT else HT + j

        def below(i):
            found = []
            n = min(HT, NT - 1 - i)
            if n:
                e0 = block(NT - 1, i)
                found.append((0, 0, n, energy[:, e0:e0 + (NT + 2) * (n - 1) + 1:NT + 2, :], p_below[:, 0:n, :]))
            n = HT - 1 - i
            if n > 0:
                e0 = block(i + 1, i)
                found.append((1, slot(i + 1), n, energy[:, e0:e0 + (NT + 1) * (n - 1) + 1:NT + 1, :], p_right[:, i:HT - 1, :]))
            return found

        def total_of(i):
            return energy[:, block(i, i), :], p_below[:, 1, :]

        def sums(i):
            return sum(len(below(k)) for k in range(i + 1))

        def left(i, h):
            js = sorted((j for j in range(i + 1) if slot(j) // HT == h), key=slot)
            return (slot(js[0]), js) if js else (0, [])

        def pt_events(i, h):
            return i + max(0, i - HT) + (i >= HT) + h

        x_dma = [sem(f"x_dma{n}") for n in range(4)]
        x_stats = sem("x_stats")
        x_norm = sem("x_norm")
        xs_done = sem("xs_done")
        xh_done = sem("xh_done")
        xl_done = sem("xl_done")
        xt_t = sem("xt_t")
        xth_done = sem("xth_done")
        xtl_done = sem("xtl_done")
        e_ps = sem("e_ps")
        e_kept = sem("e_kept")
        a_dma = sem("a_dma")
        b_dma = sem("b_dma")
        w_dma = [sem("w_dma0"), sem("w_dma1")]
        ah_done = sem("ah_done")
        al_done = sem("al_done")
        bt_t = sem("bt_t")
        bth_done = sem("bth_done")
        bt_done = sem("bt_done")
        lora_ps = sem("lora_ps")
        weff_done = sem("weff_done")
        wt_t = sem("wt_t")
        wh_done = sem("wh_done")
        wl_done = sem("wl_done")
        cmin_done = sem("cmin_done")
        cmin_t = sem("cmin_t")
        rmin_t = sem("rmin_t")
        diff_done = sem("diff_done")
        eb_done = sem("eb_done")
        exp_done = sem("exp_done")
        expt_done = sem("expt_done")
        csum_done = sem("csum_done")
        sum_t = sem("sum_t")
        pt_t = sem("pt_t")
        pth_done = sem("pth_done")
        ptl_done = sem("ptl_done")
        coef_done = sem("coef_done")
        pv_half = sem("pv_half")
        r_dma = [sem("r_dma0"), sem("r_dma1")]
        xs2_done = sem("xs2_done")
        att_evac = sem("att_evac")
        att_stats = sem("att_stats")
        att_norm = sem("att_norm")
        n_done = sem("n_done")
        x1_done = sem("x1_done")
        x1_stats = sem("x1_stats")
        x1_norm = sem("x1_norm")
        x2_done = sem("x2_done")
        x2t_t = sem("x2t_t")
        x2h_done = sem("x2h_done")
        x2l_done = sem("x2l_done")
        ffn_done = sem("ffn_done")
        y_evac = sem("y_evac")
        y_stats = sem("y_stats")
        y_norm = sem("y_norm")
        yn_done = sem("yn_done")
        out_ready = sem("out_ready")
        out_dma = sem("out_dma")
        bn_done = [sem(f"bn_done_{k}") for k in "xary"]
        veps_done = [sem(f"veps_done_{k}") for k in "xary"]
        r_done = [sem(f"r_done_{k}") for k in "xary"]
        emin_done = sem("emin_done")
        rmin_done = sem("rmin_done")
        rsum_done = sem("rsum_done")
        rinv_done = sem("rinv_done")
        const_dma = sem("const_dma")
        ident_zero = sem("ident_zero")
        const_ready = sem("const_ready")
        const_step = sem("const_step")
        bias_ready = sem("bias_ready")

        per_batch = {
            e_ps: ECHUNKS, e_kept: ECHUNKS, a_dma: DMA, ah_done: 1, al_done: 1, bt_t: 1, bth_done: 1, bt_done: 1,
            lora_ps: 2 * NK, weff_done: 2 * NK, wt_t: 2 * NK, wh_done: 2 * NK, wl_done: 2 * NK,
            cmin_done: NT - 1, cmin_t: NT - 1, rmin_t: NT - 1, diff_done: NT - 1, expt_done: NT - 1, csum_done: sums(NT - 2), sum_t: NT - 1,
            emin_done: NT - 1, pt_t: pt_events(NT - 1, 1), pth_done: 2 * NT, ptl_done: 2 * NT, pv_half: 2 * NT, ffn_done: 2 * NT, y_evac: 2 * NT,
            out_dma: DMA * NT,
        }
        for pair, n in ((x_dma, NT // 4), (r_dma, HT), (w_dma, NK // 2)):
            per_batch.update({one: DMA * n for one in pair})
        primed = (y_evac, out_dma)

        XN, AN, RN, YN = range(4)

        def counts(b):
            def at(which, n):
                per = per_batch.get(which, NT)
                assert 0 <= n <= per, n
                return b * per + (n + 1 if which in primed else n)
            return at

        block_of = ctx.enter_context(nc.Block())

        @block_of.sync
        def _(sp):
            sp.sem_inc(out_dma, 1)

            def load_x(t, b, at, buffers=2):
                if t >= buffers:
                    sp.wait_ge(xs_done, at(xs_done, t + 1 - buffers))
                sp.dma_start(x_in[t % 2], x_tiles[bass.ds(b * NT + t, 1), :, :].rearrange("a p d -> (a p) d"))\
                  .then_inc(x_dma[t % 4], DMA)

            for t in range(HEAD):
                sp.dma_start(x_first[t], x_tiles[t]).then_inc(x_dma[t % 4], DMA)
            sp.dma_start(starts_i[:, :], starts.rearrange("(a n) -> a n", a=1).to_broadcast([KR, NSTART])).then_inc(const_dma, DMA)
            sp.dma_start(gamma_b[:, :], gamma.rearrange("(a n) -> a n", a=1).to_broadcast([P, 1])).then_inc(const_dma, DMA)
            sp.dma_start(bias_b[:, :], bias.rearrange("(a n) -> a n", a=1).to_broadcast([P, D])).then_inc(const_dma, DMA)
            for t in range(HEAD, HEAD + 2):
                load_x(t, 0, counts(0), buffers=4)
            for a in range(NA):
                sp.dma_start(b_raw[:, :, a * R:(a + 1) * R], lora_b[a].rearrange("(t p) r -> p t r", p=P)).then_inc(b_dma, DMA)
            with sp.Fori(0, NB) as b:
                at = counts(b)
                for t in range(HEAD + 2, NT):
                    load_x(t, b, at)
                sp.wait_ge(e_ps, at(e_ps, ECHUNKS))
                sp.dma_start(a_mat, lora_a.rearrange("a r d -> (a r) d")).then_inc(a_dma, DMA)

                def load_w(w):
                    if w >= 2:
                        sp.wait_ge(wt_t, at(wt_t, 2 * (w - 1)))
                    sp.dma_start(w_stage[w % 2], weight[w * P:(w + 1) * P, :]).then_inc(w_dma[w % 2], DMA)

                def load_row(i):
                    if i == 1:
                        sp.wait_ge(al_done, at(al_done, 1))
                    sp.dma_start(x1[:, i % 2, :], x_tiles[bass.ds(b * NT + i, 1), :, :].rearrange("a p d -> (a p) d"))\
                      .then_inc(r_dma[i % 2], DMA)

                def store(i):
                    sp.wait_ge(out_ready, at(out_ready, i + 1))
                    sp.dma_start(out_tiles[bass.ds(b * NT + i, 1), :, :].rearrange("a p d -> (a p) d"), y)\
                      .then_inc(out_dma, DMA)

                load_w(0)
                load_w(1)
                load_row(0)
                for w in range(2, NK):
                    load_w(w)
                load_row(1)
                for i in range(NT - 3):
                    store(i)
                    load_row(i + 2)
                with sp.If(b < LAST):
                    sp.wait_ge(pt_t, at(pt_t, pt_events(NT - 1, 1)))
                    for t in range(2):
                        load_x(t, LAST, counts(LAST))
                store(NT - 3)
                load_row(NT - 1)
                with sp.If(b < LAST):
                    for t in range(2, HEAD):
                        load_x(t, LAST, counts(LAST))
                store(NT - 2)
                with sp.If(b < LAST):
                    for t in range(HEAD, HEAD + 2):
                        load_x(t, LAST, counts(LAST))
                store(NT - 1)
            sp.wait_ge(out_dma, NB * per_batch[out_dma] + 1)

        @block_of.tensor
        def _(pe):
            pe.wait_ge(const_ready, 2)

            def product(ps, left, right, first, last):
                for n, (u, v) in enumerate(((0, 0), (0, 1), (1, 0))):
                    mm = nc.tensor.matmul(ps, left[u], right[v], start=first and n == 0, stop=last and n == 2)
                return mm

            def transpose_x(t, at):
                pe.wait_ge(xs_done, at(xs_done, t + 1))
                if t == HEAD:
                    pe.wait_ge(y_evac, at(y_evac, 0))
                elif t >= 2:
                    pe.wait_ge(xtl_done, at(xtl_done, t - 1))
                for k in range(NK):
                    tr = nc.tensor.transpose(ps_xt[t][:, k * P:(k + 1) * P], xs[t % 2][:, k * P:(k + 1) * P], ident[:, :])
                tr.then_inc(xt_t, 1)

            def energy_chunk(j, c, at, beside=None):
                n, done = min(4, j + 1 - 4 * c), chunk_number(j, c)
                if done >= 4:
                    pe.wait_ge(e_kept, at(e_kept, done - 3))
                bank = ps_a[:, (done % 4) * BANK:(done % 4) * BANK + n * P]
                for k in range(NK):
                    mm = product(bank, [xt[:, j, u, k, :] for u in range(2)],
                                 [xt[:, 4 * c:4 * c + n, u, k, :] for u in range(2)], k == 0, k == NK - 1)
                    if beside and k == 2:
                        beside(0)
                mm.then_inc(e_ps, 1)

            def energy_row(j, at):
                pe.wait_ge(xtl_done, at(xtl_done, HEAD if j == 2 else j + 1))
                for c in range(chunks(j)):
                    energy_chunk(j, c, at)

            transpose_x(0, counts(0))
            transpose_x(1, counts(0))
            transpose_x(2, counts(0))
            energy_row(0, counts(0))
            transpose_x(3, counts(0))
            energy_row(1, counts(0))
            energy_row(2, counts(0))
            with pe.Fori(0, NB) as b:
                at = counts(b)

                def transpose_b():
                    pe.wait_ge(b_dma, NA * DMA)
                    pe.wait_ge(ptl_done, at(ptl_done, 2))
                    pe.nop(nofuse=True)
                    for t in range(NK):
                        tr = nc.tensor.transpose(ps_c[0:KR, t * P:(t + 1) * P], b_raw[:, t, :], ident[:, :])
                    tr.then_inc(bt_t, 1)

                def lora(q):
                    w, h = q // 2, q % 2
                    if q == 0:
                        pe.wait_ge(bt_done, at(bt_done, 1))
                        pe.wait_ge(al_done, at(al_done, 1))
                    elif q > 1:
                        pe.wait_ge(wl_done, at(wl_done, q - 1))
                    product(ps_c[:, h * BANK:(h + 1) * BANK], [bt[:, u, w * P:(w + 1) * P] for u in range(2)],
                            [a_split[:, u, h * NK // 2:(h + 1) * NK // 2, :] for u in range(2)], True, True).then_inc(lora_ps, 1)

                def transpose_w(q):
                    w, h = q // 2, q % 2
                    pe.wait_ge(weff_done, at(weff_done, q + 1))
                    for k in range(h * HT // 2, (h + 1) * HT // 2):
                        tr = nc.tensor.transpose(ps_c[:, k * P:(k + 1) * P], w_stage[w % 2][:, k * P:(k + 1) * P], ident[:, :])
                    tr.then_inc(wt_t, 1)

                def due(products):
                    return min(max(products, 0) * (2 * NK + 1) // (2 * NT - 6), 2 * NK + 1)

                def prepare_weight(q):
                    if q:
                        transpose_w(q - 1)
                    if q < 2 * NK:
                        lora(q)

                def transpose_column_min(i):
                    if i == 0:
                        pe.wait_ge(cmin_done, at(cmin_done, 1))
                        pe.wait_ge(e_kept, at(e_kept, ECHUNKS - 3))
                        nc.tensor.transpose(ps_row(0, 2, 1), energy[:, block(NT - 1, 0), :], ident[:, :])
                    else:
                        pe.wait_ge(ptl_done, at(ptl_done, 2 * i))
                        if i == 1:
                            pe.wait_ge(e_kept, at(e_kept, ECHUNKS))
                        if i == NT - 1:
                            return
                        pe.wait_ge(cmin_done, at(cmin_done, i + 1))
                    for n, _ in enumerate(below(i)):
                        tr = nc.tensor.transpose(ps_row(i, n, 1), col_min[:, n, :], ident[:, :])
                    tr.then_inc(cmin_t, 1)

                def spread_row_min(i):
                    pe.wait_ge(rmin_done, at(rmin_done, i + 1))
                    nc.tensor.transpose(ps_row(i, 4, 1), rmin[:, i:i + 1].to_broadcast([P, P]), ident[:, :]).then_inc(rmin_t, 1)

                def transpose_p(i, h):
                    place, js = left(i, h)
                    if not js:
                        return
                    pe.wait_ge(exp_done, at(exp_done, i + 1))
                    if i < NT - 1:
                        pe.wait_ge(diff_done, at(diff_done, i + 1))
                    if h and i:
                        pe.wait_ge(rsum_done, at(rsum_done, i))
                    for n, j in enumerate(js):
                        tr = nc.tensor.transpose(ps_row(i, place + n, 1), energy[:, block(i, j), :], ident[:, :])
                    tr.then_inc(pt_t, 1)

                def sum_below(i):
                    if i == NT - 1:
                        return
                    pe.wait_ge(csum_done, at(csum_done, sums(i)))
                    for n in range(len(below(i))):
                        mm = nc.tensor.matmul(ps_a[:, 12 * P:12 * P + 1], total_of(i)[n], ones[:, :], start=n == 0, stop=n == len(below(i)) - 1)
                    mm.then_inc(sum_t, 1)

                def attend(i, h):
                    pe.wait_ge(ptl_done, at(ptl_done, 2 * i + h + 1))
                    if h == 0:
                        if i:
                            pe.wait_ge(att_evac, at(att_evac, i))
                        else:
                            pe.wait_ge(xl_done, at(xl_done, NT))
                    for q in range(h * HT, (h + 1) * HT):
                        j = NT - 1 - q if q < HT else q - HT
                        for c in range(2):
                            mm = product(ps_b[:, c * BANK:(c + 1) * BANK], [pt[:, u, q, :] for u in range(2)],
                                         [z[:, j, c * BANK:(c + 1) * BANK] for z in (x_high, x_low)], q == 0, q == NT - 1)
                            done = 2 * (q - 2) + c
                            if i == 0 and due(done) < due(done + 1):
                                prepare_weight(due(done))
                        if q == (h + 1) * HT - 1:
                            mm.then_inc(pv_half, 1)
                        if q == 1 and 0 < i < NT - 1:
                            transpose_column_min(i + 1)
                        if q == (3 if i else 2):
                            sum_below(i)
                            if i + 1 < NT - 1:
                                spread_row_min(i + 1)
                        if i == 0 and q == 0:
                            transpose_column_min(1)
                            transpose_b()

                def transpose_x2(i):
                    pe.wait_ge(x2_done, at(x2_done, i + 1))
                    if i:
                        pe.wait_ge(y_evac, at(y_evac, 2 * i))
                    else:
                        pe.wait_ge(wl_done, at(wl_done, 2 * NK))
                    for k in range(NK):
                        tr = nc.tensor.transpose(ps_c[:, k * P:(k + 1) * P], att[:, k * P:(k + 1) * P], ident[:, :])
                    tr.then_inc(x2t_t, 1)

                def feed_forward(i):
                    pe.wait_ge(x2l_done, at(x2l_done, i + 1))
                    for c in range(2):
                        for k in range(NK):
                            mm = product(ps_c[:, c * BANK:(c + 1) * BANK], [x2t[:, u, k, :] for u in range(2)],
                                         [wt[:, u, k, c * BANK:(c + 1) * BANK] for u in range(2)], k == 0, k == NK - 1)
                        mm.then_inc(ffn_done, 1)

                for kind, n in order[:-1]:
                    if kind == "T":
                        transpose_x(n, at)
                    else:
                        energy_row(n, at)
                pe.wait_ge(xtl_done, at(xtl_done, NT))
                energy_chunk(NT - 1, 0, at)
                energy_chunk(NT - 1, 1, at)
                transpose_column_min(0)
                energy_chunk(NT - 1, 2, at, beside=spread_row_min)
                transpose_p(0, 1)
                energy_chunk(NT - 1, 3, at)
                for i in range(NT):
                    attend(i, 0)
                    if i + 1 < NT:
                        transpose_p(i + 1, 0)
                    if i:
                        transpose_x2(i - 1)
                    attend(i, 1)
                    if i + 1 < NT:
                        transpose_p(i + 1, 1)
                    if i:
                        feed_forward(i - 1)
                with pe.If(b < LAST):
                    pe.wait_ge(att_evac, at(att_evac, NT))
                    transpose_x(0, counts(LAST))
                    transpose_x(1, counts(LAST))
                transpose_x2(NT - 1)
                with pe.If(b < LAST):
                    transpose_x(2, counts(LAST))
                    energy_row(0, counts(LAST))
                feed_forward(NT - 1)
                with pe.If(b < LAST):
                    transpose_x(3, counts(LAST))
                    energy_row(1, counts(LAST))
                    energy_row(2, counts(LAST))

        @block_of.vector
        def _(dve):
            dve.sem_inc(y_evac, 1)

            def row_stats(kind, n, rows, done, at, halves=(0, 1)):
                for c in halves:
                    part_stats = nc.vector.bn_stats(bn[:, kind, c, :], rows[:, c * BANK:(c + 1) * BANK])
                if 1 not in halves:
                    return
                part_stats.then_inc(bn_done[kind], 1)
                dve.wait_ge(bn_done[kind], at(bn_done[kind], n + 1))
                dve.nop(nofuse=True)
                nc.vector.bn_aggr(mv[:, kind, :], bn[:, kind, :, :]).then_inc(done, 1)

            def stats_x(t, at, rows=None):
                dve.wait_ge(x_dma[t % 4], at(x_dma[t % 4], DMA * (t // 4 + 1)))
                if t:
                    dve.wait_ge(x_norm, at(x_norm, t))
                row_stats(XN, t, x_in[t % 2] if rows is None else rows, x_stats, at)

            def split_xt(t, at):
                dve.wait_ge(xth_done, at(xth_done, t + 1))
                nc.vector.tensor_tensor(xt[:, t, 1, :, :].rearrange("p k n -> p (k n)"), ps_xt[t][:, :],
                                        xt[:, t, 0, :, :].rearrange("p k n -> p (k n)"), ALU.subtract).then_inc(xtl_done, 1)

            def keep_chunk(j, c, at):
                n, done = min(4, j + 1 - 4 * c), chunk_number(j, c)
                dve.wait_ge(e_ps, at(e_ps, done + 1))
                place = block(j, 4 * c)
                nc.vector.tensor_scalar(flat[:, place * P:(place + n) * P], ps_a[:, (done % 4) * BANK:(done % 4) * BANK + n * P],
                                        1.0, None, ALU.mult, ALU.min, accum_out=emin[:, j, c:c + 1]).then_inc(e_kept, 1)

            def keep_energy(j, at):
                if j >= NT - 3:
                    dve.wait_ge(xt_t, at(xt_t, min(j + 2, NT)))
                    dve.wait_ge(xl_done, at(xl_done, min(j + 2, NT)))
                for c in range(chunks(j)):
                    keep_chunk(j, c, at)

            for t in range(3):
                stats_x(t, counts(0), x_first[t])
            split_xt(0, counts(0))
            stats_x(3, counts(0), x_first[3])
            split_xt(1, counts(0))
            stats_x(HEAD, counts(0))
            split_xt(2, counts(0))
            keep_energy(0, counts(0))
            split_xt(3, counts(0))
            stats_x(HEAD + 1, counts(0))
            keep_energy(1, counts(0))
            keep_energy(2, counts(0))

            count = [0]

            dve.wait_ge(const_dma, 3 * DMA)
            dve.wait_ge(const_ready, 2)

            def const(ins):
                count[0] += 1
                ins.then_inc(const_step, 1)
                dve.wait_ge(const_step, count[0])

            const(nc.vector.tensor_copy(starts_f[:, :], starts_i[:, :]))
            for n in range(NB):
                lo, hi = is_below[:, n, :], seg[:, n, :]
                const(nc.vector.tensor_scalar(lo, starts_f[:, :], float(n), None, ALU.is_le))
                const(nc.vector.tensor_scalar(hi[:, 0:1], lo[:, 0:1], -1.0, 2.0, ALU.mult, ALU.add))
                const(nc.vector.scalar_tensor_tensor(hi[:, 1:2], hi[:, 0:1], lo[:, 1:2], lo[:, 0:1], ALU.mult, ALU.add))
                const(nc.vector.scalar_tensor_tensor(hi[:, 2:3], lo[:, 3:4], 3.0, hi[:, 1:2], ALU.add, ALU.subtract))
                const(nc.vector.scalar_tensor_tensor(hi[:, 3:4], hi[:, 2:3], lo[:, 2:3], hi[:, 1:2], ALU.mult, ALU.add))
                const(nc.vector.scalar_tensor_tensor(hi[:, 0:1], hi[:, 3:4], -float(R), row_id[:, :], ALU.mult, ALU.add))
                const(nc.vector.tensor_scalar(hi[:, 1:2], hi[:, 0:1], -2.0 * R, None, ALU.is_ge))
                const(nc.vector.scalar_tensor_tensor(hi[:, 2:3], hi[:, 0:1], float(-R), hi[:, 1:2], ALU.is_lt, ALU.mult))
                const(nc.vector.tensor_scalar(mask[:, n:n + 1], hi[:, 2:3], LS, None, ALU.mult))
            nc.vector.tensor_scalar(bias_b[:, :], bias_b[:, :], XS * WS, None, ALU.mult).then_inc(bias_ready, 1)
            dve.wait_ge(bias_ready, 1)

            with dve.Fori(0, NB) as b:
                at = counts(b)
                for kind, n in order[:-1]:
                    if kind == "T":
                        split_xt(n, at)
                        if n + 2 < NT:
                            stats_x(n + 2, at)
                    else:
                        keep_energy(n, at)
                dve.wait_ge(e_kept, at(e_kept, ECHUNKS - 4))

                def column_minimum(i, pieces=(0, 1)):
                    if i >= NT - 1:
                        return
                    for n, (_, _, _, e, _) in enumerate(below(i)):
                        if n not in pieces:
                            continue
                        if i == 0 and n == 0:
                            e = e[:, 1:HT, :]
                        m = nc.vector.tensor_reduce(col_min[:, n, :], e.rearrange("p j n -> p n j"), AX.X, ALU.min)
                    if len(below(i)) - 1 in pieces:
                        m.then_inc(cmin_done, 1)

                def row_minimum(i):
                    parts = chunks(i)
                    if i < NT - 1:
                        dve.wait_ge(cmin_t, at(cmin_t, i + 1))
                        nc.vector.tensor_reduce(emin[:, i, parts:parts + 1], ps_row(i, 0, len(below(i)) + (i == 0)), AX.X, ALU.min)\
                          .then_inc(emin_done, 1)
                        parts += 1
                        dve.wait_ge(emin_done, at(emin_done, i + 1))
                    else:
                        dve.wait_ge(e_kept, at(e_kept, ECHUNKS))
                    nc.vector.tensor_reduce(rmin[:, i:i + 1], emin[:, i, 0:parts], AX.X, ALU.min).then_inc(rmin_done, 1)
                    dve.wait_ge(rmin_done, at(rmin_done, i + 1))
                    nc.vector.tensor_scalar(ebias[:, i:i + 1], rmin[:, i:i + 1], 1.0 / (XS * XS), LN14, ALU.mult, ALU.add)\
                      .then_inc(eb_done, 1)

                def less_minimum(i, pieces=(0, 1)):
                    if i == NT - 1:
                        return
                    dve.wait_ge(rmin_t, at(rmin_t, i + 1))
                    for half, (_, _, n, e, p) in enumerate(below(i)):
                        if half not in pieces:
                            continue
                        m = nc.vector.tensor_tensor(p, e, ps_row(i, 4, 1).rearrange("p (j n) -> p j n", j=1).to_broadcast([P, n, P]),
                                                    ALU.subtract)
                    if len(below(i)) - 1 in pieces:
                        m.then_inc(diff_done, 1)

                def coefficient(i):
                    dve.wait_ge(exp_done, at(exp_done, i + 1))
                    if i < NT - 1:
                        dve.wait_ge(sum_t, at(sum_t, i + 1))
                        nc.vector.tensor_tensor(rsum[:, i % 2:i % 2 + 1], ps_a[:, 12 * P:12 * P + 1], esum[:, i:i + 1], ALU.add).then_inc(rsum_done, 1)
                    else:
                        nc.vector.tensor_copy(rsum[:, i % 2:i % 2 + 1], esum[:, i:i + 1]).then_inc(rsum_done, 1)
                    dve.wait_ge(rsum_done, at(rsum_done, i + 1))
                    nc.vector.reciprocal(rinv[:, i % 2:i % 2 + 1], rsum[:, i % 2:i % 2 + 1]).then_inc(rinv_done, 1)
                    dve.wait_ge(rinv_done, at(rinv_done, i + 1))
                    nc.vector.tensor_tensor(coef[:, i % 2:i % 2 + 1], rinv[:, i % 2:i % 2 + 1], gamma_b[:, :], ALU.mult).then_inc(coef_done, 1)

                def split_pt(i, h):
                    dve.wait_ge(pth_done, at(pth_done, 2 * i + h + 1))
                    place, js = left(i, h)
                    parts = [(place, len(js), ps_row(i, place, len(js)).rearrange("p (j n) -> p j n", n=P))] if js else []
                    parts += [(p0, n, p) for half, p0, n, _, p in below(i) if half == h]
                    for p0, n, source in parts:
                        low = nc.vector.tensor_tensor(pt[:, 1, p0:p0 + n, :], source, pt[:, 0, p0:p0 + n, :], ALU.subtract)
                    low.then_inc(ptl_done, 1)

                def column_sum(i):
                    if i == NT - 1:
                        return
                    dve.wait_ge(ptl_done, at(ptl_done, 2 * i + 2))
                    for n, (_, _, _, _, p) in enumerate(below(i)):
                        if n:
                            dve.wait_ge(csum_done, at(csum_done, sums(i) - 1))
                        nc.vector.tensor_reduce(total_of(i)[n], p.rearrange("p j n -> p n j"), AX.X, ALU.add).then_inc(csum_done, 1)

                def split_adapters():
                    a_in = a_mat.rearrange("r (k n) -> r k n", k=NK)
                    dve.wait_ge(a_dma, at(a_dma, DMA))
                    nc.vector.tensor_scalar(a_split[:, 0, :, :], a_in, mask[:, bass.ds(b, 1)], None, ALU.mult).then_inc(ah_done, 1)
                    dve.wait_ge(ah_done, at(ah_done, 1))
                    nc.vector.scalar_tensor_tensor(a_split[:, 1, :, :], a_in, mask[:, bass.ds(b, 1)], a_split[:, 0, :, :],
                                                   ALU.mult, ALU.subtract).then_inc(al_done, 1)
                    dve.wait_ge(bth_done, at(bth_done, 1))
                    nc.vector.scalar_tensor_tensor(bt[:, 1, :], ps_c[0:KR, :], LS, bt[:, 0, :], ALU.mult, ALU.subtract)\
                      .then_inc(bt_done, 1)

                def add_adapter(q):
                    w, h = q // 2, q % 2
                    dve.wait_ge(w_dma[w % 2], at(w_dma[w % 2], DMA * (w // 2 + 1)))
                    dve.wait_ge(lora_ps, at(lora_ps, q + 1))
                    half = w_stage[w % 2][:, h * BANK:(h + 1) * BANK]
                    nc.vector.scalar_tensor_tensor(half, ps_c[:, h * BANK:(h + 1) * BANK], LS ** -2, half, ALU.mult, ALU.add)\
                      .then_inc(weff_done, 1)

                def split_weight(q):
                    w, k = q // 2, q % 2 * (NK // 2)
                    dve.wait_ge(wh_done, at(wh_done, q + 1))
                    nc.vector.scalar_tensor_tensor(wt[:, 1, k:k + NK // 2, w * P:(w + 1) * P],
                                                   ps_c[:, k * P:k * P + BANK].rearrange("p (k n) -> p k n", k=NK // 2), WS,
                                                   wt[:, 0, k:k + NK // 2, w * P:(w + 1) * P], ALU.mult, ALU.subtract).then_inc(wl_done, 1)

                def prepare_weight(first, end):
                    for q in range(first, end):
                        if q < 2 * NK:
                            add_adapter(q)
                        if q:
                            split_weight(q - 1)

                def attended(i):
                    dve.wait_ge(pv_half, at(pv_half, 2 * i + 2))
                    dve.wait_ge(xs2_done, at(xs2_done, i + 1))
                    dve.wait_ge(coef_done, at(coef_done, i + 1))
                    nc.vector.scalar_tensor_tensor(att, ps_b[:, :], coef[:, i % 2:i % 2 + 1], att, ALU.mult, ALU.add)\
                      .then_inc(att_evac, 1)
                    dve.wait_ge(att_evac, at(att_evac, i + 1))
                    if i:
                        dve.wait_ge(att_norm, at(att_norm, i))
                    row_stats(AN, i, att, att_stats, at)

                def stats_x1(i):
                    dve.wait_ge(x1_done, at(x1_done, i + 1))
                    if i:
                        dve.wait_ge(x1_norm, at(x1_norm, i))
                    row_stats(RN, i, x1[:, i % 2, :], x1_stats, at)

                def split_x2(i):
                    dve.wait_ge(x2h_done, at(x2h_done, i + 1))
                    nc.vector.tensor_tensor(x2t[:, 1, :, :].rearrange("p k n -> p (k n)"), ps_c[:, :],
                                            x2t[:, 0, :, :].rearrange("p k n -> p (k n)"), ALU.subtract).then_inc(x2l_done, 1)

                def evacuate_y(i, c):
                    dve.wait_ge(ffn_done, at(ffn_done, 2 * i + c + 1))
                    if i and c == 0:
                        dve.wait_ge(out_dma, at(out_dma, DMA * i))
                        dve.wait_ge(y_norm, at(y_norm, i))
                    half = slice(c * BANK, (c + 1) * BANK)
                    nc.vector.tensor_tensor(y[:, half], ps_c[:, half], bias_b[:, half], ALU.add).then_inc(y_evac, 1)

                def stats_y(i, halves=(0, 1)):
                    dve.wait_ge(y_evac, at(y_evac, 2 * i + 1 + max(halves)))
                    row_stats(YN, i, y, y_stats, at, halves)

                def measure_y(i):
                    evacuate_y(i, 0)
                    evacuate_y(i, 1)
                    stats_y(i)

                column_minimum(0)
                keep_chunk(NT - 1, 0, at)
                keep_chunk(NT - 1, 1, at)
                row_minimum(0)
                column_minimum(1)
                less_minimum(0)
                keep_chunk(NT - 1, 2, at)
                split_pt(0, 0)
                split_pt(0, 1)
                keep_chunk(NT - 1, 3, at)
                column_sum(0)
                split_adapters()
                for i in range(NT - 1):
                    row_minimum(i + 1)
                    coefficient(i)
                    if i >= 2:
                        measure_y(i - 2)
                    if i == 1:
                        stats_x1(0)
                    if i:
                        less_minimum(i + 1)
                        column_minimum(i + 2)
                    else:
                        for n in range(2):
                            prepare_weight(n, n + 1)
                            less_minimum(1, [n])
                        for n in range(2):
                            prepare_weight(n + 2, n + 3)
                            column_minimum(2, [n])
                        prepare_weight(4, HT - 1)
                    split_pt(i + 1, 0)
                    if i:
                        split_x2(i - 1)
                    else:
                        prepare_weight(HT - 1, 2 * NK + 1)
                    attended(i)
                    split_pt(i + 1, 1)
                    column_sum(i + 1)
                    if i:
                        stats_x1(i)
                measure_y(NT - 3)
                split_x2(NT - 2)
                coefficient(NT - 1)
                with dve.If(b < LAST):
                    stats_x(0, counts(LAST))
                    stats_x(1, counts(LAST))
                attended(NT - 1)
                with dve.If(b < LAST):
                    stats_x(2, counts(LAST))
                dve.wait_ge(n_done, at(n_done, NT))
                nc.vector.tensor_tensor(x1[:, (NT - 1) % 2, :], x1[:, (NT - 1) % 2, :], att, ALU.add).then_inc(x1_done, 1)
                stats_x1(NT - 1)
                measure_y(NT - 2)
                with dve.If(b < LAST):
                    split_xt(0, counts(LAST))
                    stats_x(3, counts(LAST))
                split_x2(NT - 1)
                with dve.If(b < LAST):
                    keep_energy(0, counts(LAST))
                    split_xt(1, counts(LAST))
                    split_xt(2, counts(LAST))
                    stats_x(4, counts(LAST))
                evacuate_y(NT - 1, 0)
                stats_y(NT - 1, [0])
                evacuate_y(NT - 1, 1)
                with dve.If(b < LAST):
                    split_xt(3, counts(LAST))
                stats_y(NT - 1, [1])
                with dve.If(b < LAST):
                    stats_x(HEAD + 1, counts(LAST))
                    keep_energy(1, counts(LAST))
                    keep_energy(2, counts(LAST))
                dve.wait_ge(yn_done, at(yn_done, NT))
                nc.vector.tensor_tensor(y, x1[:, (NT - 1) % 2, :], y, ALU.add).then_inc(out_ready, 1)

        @block_of.scalar
        def _(act):
            def norm_x(t, at, rows=None):
                act.wait_ge(x_norm, at(x_norm, t + 1))
                if t >= 2:
                    act.wait_ge(xt_t, at(xt_t, t - 1))
                    act.wait_ge(xl_done, at(xl_done, t - 1))
                nc.scalar.activation(xs[t % 2], x_in[t % 2] if rows is None else rows, ACT.Identity, bias=x_nb[:, t:t + 1], scale=x_r[:, t:t + 1])\
                  .then_inc(xs_done, 1)

            def high_x(t, at):
                act.wait_ge(xs_done, at(xs_done, t + 1))
                nc.scalar.activation(x_high[:, t, :], xs[t % 2], ACT.Copy).then_inc(xh_done, 1)

            def split_xt(t, at):
                act.wait_ge(xt_t, at(xt_t, t + 1))
                if t == NT - 3:
                    act.wait_ge(out_dma, at(out_dma, 0))
                nc.scalar.activation(xt[:, t, 0, :, :].rearrange("p k n -> p (k n)"), ps_xt[t][:, :], ACT.Copy)\
                  .then_inc(xth_done, 1)

            act.wait_ge(const_ready, 2)
            nc.scalar.activation(esum[:, 0:1], neg_half[:, :], ACT.Exp)
            norm_x(0, counts(0), x_first[0])
            for t in range(HEAD):
                high_x(t, counts(0))
                if t + 1 < HEAD:
                    norm_x(t + 1, counts(0), x_first[t + 1])
                split_xt(t, counts(0))
            norm_x(HEAD, counts(0))
            high_x(HEAD, counts(0))
            with act.Fori(0, NB) as b:
                at = counts(b)
                for kind, t in order:
                    if kind == "T":
                        split_xt(t, at)
                        if t + 1 < NT:
                            norm_x(t + 1, at)
                            high_x(t + 1, at)

                def exponentials(i):
                    act.wait_ge(eb_done, at(eb_done, i + 1))
                    row = flat[:, block(i, 0) * P:(block(i, 0) + i + 1) * P]
                    nc.scalar.activation(row, row, ACT.Exp, bias=ebias[:, i:i + 1], scale=-1.0 / (XS * XS),
                                         accum_out=esum[:, i:i + 1]).then_inc(exp_done, 1)

                def exponentials_below(i):
                    if i == NT - 1:
                        return
                    act.wait_ge(diff_done, at(diff_done, i + 1))
                    for _, _, _, _, p in below(i):
                        e = nc.scalar.activation(p, p, ACT.Exp, bias=ln14[:, 0:1], scale=-1.0 / (XS * XS))
                    e.then_inc(expt_done, 1)

                def split_pt(i, h):
                    place, js = left(i, h)
                    parts = []
                    if js:
                        act.wait_ge(pt_t, at(pt_t, pt_events(i, h)))
                        parts.append((place, len(js), ps_row(i, place, len(js)).rearrange("p (j n) -> p j n", n=P)))
                    if i < NT - 1:
                        act.wait_ge(expt_done, at(expt_done, i + 1))
                    if i:
                        act.wait_ge(pv_half, at(pv_half, 2 * i - 1 + h))
                    parts += [(p0, n, p) for half, p0, n, _, p in below(i) if half == h]
                    for p0, n, source in parts:
                        high = nc.scalar.activation(pt[:, 0, p0:p0 + n, :], source, ACT.Copy)
                    high.then_inc(pth_done, 1)

                def high_weight(first, end):
                    for q in range(first, end):
                        w, k = q // 2, q % 2 * (NK // 2)
                        act.wait_ge(wt_t, at(wt_t, q + 1))
                        if q == 0:
                            act.wait_ge(e_ps, at(e_ps, ECHUNKS))
                        nc.scalar.activation(wt[:, 0, k:k + NK // 2, w * P:(w + 1) * P],
                                             ps_c[:, k * P:k * P + BANK].rearrange("p (k n) -> p k n", k=NK // 2), ACT.Copy,
                                             scale=WS).then_inc(wh_done, 1)

                def norm_rows(i):
                    act.wait_ge(r_dma[i % 2], at(r_dma[i % 2], DMA * (i // 2 + 1)))
                    if i:
                        act.wait_ge(x2t_t, at(x2t_t, i))
                    else:
                        act.wait_ge(lora_ps, at(lora_ps, 2 * NK))
                    nc.scalar.activation(att, x1[:, i % 2, :], ACT.Identity, bias=x_nb[:, i:i + 1], scale=x_r[:, i:i + 1])\
                      .then_inc(xs2_done, 1)

                def split_x2(i):
                    act.wait_ge(x2t_t, at(x2t_t, i + 1))
                    if i:
                        act.wait_ge(ffn_done, at(ffn_done, 2 * i))
                    else:
                        act.wait_ge(wt_t, at(wt_t, 2 * NK))
                    nc.scalar.activation(x2t[:, 0, :, :].rearrange("p k n -> p (k n)"), ps_c[:, :], ACT.Copy).then_inc(x2h_done, 1)

                def norm_attended(i):
                    act.wait_ge(att_norm, at(att_norm, i + 1))
                    nc.scalar.activation(att, att, ACT.Identity, bias=ln_nb[:, 0:1], scale=ln_r[:, 0:1]).then_inc(n_done, 1)

                def norm_x1(i):
                    act.wait_ge(x1_norm, at(x1_norm, i + 1))
                    nc.scalar.activation(att, x1[:, i % 2, :], ACT.Identity, bias=ln_nb[:, 1:2], scale=ln_r[:, 1:2])\
                      .then_inc(x2_done, 1)

                def norm_y(i):
                    act.wait_ge(y_norm, at(y_norm, i + 1))
                    nc.scalar.activation(y, y, ACT.Identity, bias=ln_nb[:, 2:3], scale=ln_r[:, 2:3]).then_inc(yn_done, 1)

                exponentials(0)
                exponentials_below(0)
                split_pt(0, 0)
                split_pt(0, 1)
                act.wait_ge(bt_t, at(bt_t, 1))
                nc.scalar.activation(bt[:, 0, :], ps_c[0:KR, :], ACT.Copy, scale=LS).then_inc(bth_done, 1)
                for i in range(NT - 1):
                    exponentials(i + 1)
                    if i == 1:
                        norm_x1(0)
                    if i >= 2:
                        norm_y(i - 2)
                    if i == 0:
                        high_weight(0, 2)
                    exponentials_below(i + 1)
                    if i == 0:
                        high_weight(2, HT - 2)
                    split_pt(i + 1, 0)
                    if i:
                        split_x2(i - 1)
                    else:
                        high_weight(HT - 2, 2 * NK - 1)
                    norm_rows(i)
                    if i == 0:
                        high_weight(2 * NK - 1, 2 * NK)
                    split_pt(i + 1, 1)
                    norm_attended(i)
                    if i:
                        norm_x1(i)
                norm_y(NT - 3)
                split_x2(NT - 2)
                norm_rows(NT - 1)
                with act.If(b < LAST):
                    norm_x(0, counts(LAST))
                    norm_x(1, counts(LAST))
                norm_attended(NT - 1)
                with act.If(b < LAST):
                    act.wait_ge(pv_half, at(pv_half, 2 * NT))
                    high_x(0, counts(LAST))
                norm_x1(NT - 1)
                with act.If(b < LAST):
                    high_x(1, counts(LAST))
                    split_xt(0, counts(LAST))
                    norm_x(2, counts(LAST))
                split_x2(NT - 1)
                norm_y(NT - 2)
                with act.If(b < LAST):
                    split_xt(1, counts(LAST))
                    high_x(2, counts(LAST))
                    norm_x(3, counts(LAST))
                    split_xt(2, counts(LAST))
                    high_x(3, counts(LAST))
                    split_xt(3, counts(LAST))
                    norm_x(4, counts(LAST))
                    high_x(4, counts(LAST))
                norm_y(NT - 1)

        @block_of.gpsimd
        def _(pool):
            nc.gpsimd.memset(ident[:, :], 0.0).then_inc(ident_zero, 1)
            nc.gpsimd.memset(neg_half[:, :], -0.5)
            nc.gpsimd.memset(ones[:, :], 1.0)
            nc.gpsimd.memset(ln14[:, :], LN14)
            nc.gpsimd.iota(row_id[:, :], [[0, 1]], base=0, channel_multiplier=1, allow_small_or_imprecise_dtypes=True).then_inc(const_ready, 1)
            pool.wait_ge(ident_zero, 1)
            nc.gpsimd.affine_select(out=ident[:, :], in_=ident[:, :], compare_op=ALU.not_equal, fill=1.0,
                                    base=0, pattern=[[-1, P]], channel_multiplier=1).then_inc(const_ready, 1)
            pool.wait_ge(const_ready, 2)

            def norm(kind, n, scale, eps, r, nb, done, at):
                pool.nop(nofuse=True)
                nc.gpsimd.tensor_scalar(veps[:, kind:kind + 1], mv[:, kind, 1:2], scale, eps, ALU.mult, ALU.add)\
                  .then_inc(veps_done[kind], 1)
                pool.wait_ge(veps_done[kind], at(veps_done[kind], n + 1))
                nc.gpsimd.tensor_tensor(r, veps[:, kind:kind + 1], neg_half[:, :], ALU.pow).then_inc(r_done[kind], 1)
                pool.wait_ge(r_done[kind], at(r_done[kind], n + 1))
                pool.nop(nofuse=True)
                nc.gpsimd.tensor_scalar(nb, mv[:, kind, 0:1], r, -1.0, ALU.mult, ALU.mult).then_inc(done, 1)

            def norm_x(t, at):
                pool.wait_ge(x_stats, at(x_stats, t + 1))
                norm(XN, t, XS ** -2, EPS * XS ** -2, x_r[:, t:t + 1], x_nb[:, t:t + 1], x_norm, at)

            def low_x(t, at):
                pool.wait_ge(xh_done, at(xh_done, t + 1))
                nc.gpsimd.tensor_tensor(x_low[:, t, :], xs[t % 2], x_high[:, t, :], ALU.subtract).then_inc(xl_done, 1)

            for t in range(3):
                norm_x(t, counts(0))
            for t in range(HEAD):
                low_x(t, counts(0))
                if t % 2 == 0:
                    norm_x(3 + t // 2, counts(0))
            with pool.Fori(0, NB) as b:
                at = counts(b)
                norm_x(HEAD + 1, at)
                for t in range(HEAD, NT):
                    low_x(t, at)
                    if t + 2 < NT:
                        norm_x(t + 2, at)

                def finish_y(i):
                    pool.wait_ge(y_stats, at(y_stats, i + 1))
                    norm(YN, i, 1.0, EPS * (XS * WS) ** 2, ln_r[:, 2:3], ln_nb[:, 2:3], y_norm, at)
                    if i == NT - 1:
                        return
                    pool.wait_ge(yn_done, at(yn_done, i + 1))
                    nc.gpsimd.tensor_tensor(y, x1[:, i % 2, :], y, ALU.add).then_inc(out_ready, 1)

                def residual(i):
                    pool.wait_ge(att_stats, at(att_stats, i + 1))
                    norm(AN, i, 1.0, EPS * XS ** 2, ln_r[:, 0:1], ln_nb[:, 0:1], att_norm, at)
                    if i == NT - 1:
                        return
                    pool.wait_ge(n_done, at(n_done, i + 1))
                    nc.gpsimd.tensor_tensor(x1[:, i % 2, :], x1[:, i % 2, :], att, ALU.add).then_inc(x1_done, 1)

                def norm_residual(i):
                    pool.wait_ge(x1_stats, at(x1_stats, i + 1))
                    norm(RN, i, XS ** -2, EPS * XS ** -2, ln_r[:, 1:2], ln_nb[:, 1:2], x1_norm, at)

                for i in range(NT - 1):
                    if i >= 2:
                        finish_y(i - 2)
                    residual(i)
                    norm_residual(i)
                finish_y(NT - 3)
                with pool.If(b < LAST):
                    norm_x(0, counts(LAST))
                    norm_x(1, counts(LAST))
                residual(NT - 1)
                with pool.If(b < LAST):
                    norm_x(2, counts(LAST))
                norm_residual(NT - 1)
                with pool.If(b < LAST):
                    low_x(0, counts(LAST))
                    low_x(1, counts(LAST))
                    norm_x(3, counts(LAST))
                finish_y(NT - 2)
                with pool.If(b < LAST):
                    low_x(2, counts(LAST))
                    low_x(3, counts(LAST))
                    norm_x(4, counts(LAST))
                finish_y(NT - 1)


_INS = ["L0_attn_x", "L0_attn_gamma", "L0_ffn_weight", "L0_ffn_bias", "L0_ffn_lora_A", "L0_ffn_lora_B",
        "L0_ffn_lora_start_indices"]


def kernel(**inputs):
    import numpy as np
    import concourse.bacc as bacc
    from concourse.bass_utils import run_bass_kernel_spmd

    nc = bacc.Bacc("TRN2", target_bir_lowering=False, num_devices=1)
    arrays, args = {}, []
    for name in _INS:
        a = np.ascontiguousarray(inputs[name])
        arrays[f"in_{name}"] = a
        args.append(nc.dram_tensor(f"in_{name}", a.shape, mybir.dt.from_np(a.dtype), kind="ExternalInput").ap())
    shape = inputs["L0_attn_x"].shape
    args.append(nc.dram_tensor("out_x", shape, F32, kind="ExternalOutput").ap())
    sandwich(nc, *args)
    r = run_bass_kernel_spmd(nc, [arrays], core_ids=[0])
    return r.results[0]["out_x"]
```
